# Optimizing a Trainium2 kernel written in Bass

```python
import numpy as np
import jax
import jax.numpy as jnp

def _softmax(x, axis=-1):
    return jax.nn.softmax(x, axis=axis)

def _gelu(x):
    return jax.nn.gelu(x, approximate=True)

def _silu(x):
    return jax.nn.silu(x)

def _sigmoid(x):
    return jax.nn.sigmoid(x)

def _layernorm(x, axis=-1, eps=1e-05):
    m = jnp.mean(x, axis=axis, keepdims=True)
    v = jnp.var(x, axis=axis, keepdims=True)
    return (x - m) / jnp.sqrt(v + eps)

def _scatter_add(tgt, idx, src, axis=0):
    return tgt.at[idx].add(src)

def _segment_sum(src, seg, n):
    return jax.ops.segment_sum(src, seg, n)
kernel_name = 'mk_vit_tower_d1_tok_img1024_r4_5c4c7e'

def setup_inputs(seed: int=0):
    np.random.seed(seed)
    _w = jnp.asarray

    def _rec_inputs():
        import jax
        import jax.numpy as jnp
        _rk = jax.random.key(seed)
        x = -0.000348323 + 0.999952 * jax.random.normal(jax.random.fold_in(_rk, 1), (64, 3, 224, 224), jnp.float32)
        return x
    x = _rec_inputs()

    def _L0_tok_setup():
        import jax, jax.numpy as jnp
        import numpy as np
        from jax import lax
        PATCH = 16
        key = jax.random.key(seed)
        k1, k2 = jax.random.split(key)
        B, C, IMG, HID = (32, 3, 96, 256)
        inputs = jax.random.normal(k1, (B, C, IMG, IMG), dtype=jnp.float32)
        flat = C * PATCH * PATCH
        W = jax.random.normal(k2, (flat, HID), dtype=jnp.float32) / np.sqrt(flat)
        return {'inputs': inputs, 'W': W}
    _L0_tok_all = _L0_tok_setup()
    _L0_tok_in = {k: v for k, v in _L0_tok_all.items() if k in ('W',)}
    del _L0_tok_all

    def _L0_attn_setup():
        import jax, jax.numpy as jnp
        import numpy as np
        import math
        B, T, C = (2, 512, 256)
        H, L = (16, 64)
        DH = C // H
        DHE = DH // 2
        THETA = 10000.0

        def _rope_cache(t, dim):
            inv_freq = 1.0 / THETA ** (jnp.arange(0, dim, 2, dtype=jnp.float32) / dim)
            freqs = jnp.arange(t, dtype=jnp.float32)[:, None] * inv_freq[None, :]
            emb = jnp.concatenate((freqs, freqs), axis=-1)
            return (jnp.cos(emb), jnp.sin(emb))

        def _apply_rope(x, cos, sin):
            x1 = x[..., 0::2]
            x2 = x[..., 1::2]
            rot = jnp.stack((-x2, x1), axis=-1).reshape(x.shape)
            return x * cos[None, None] + rot * sin[None, None]
        key = jax.random.key(seed)
        ks = jax.random.split(key, 10)
        s = 0.02
        return {'x': jax.random.normal(ks[0], (B, T, C), jnp.float32), 'Wq_down': jax.random.normal(ks[1], (C, H * L), jnp.float32) * s, 'Wk_down': jax.random.normal(ks[2], (C, H * L), jnp.float32) * s, 'Wv_down': jax.random.normal(ks[3], (C, H * L), jnp.float32) * s, 'Wq_up_c': jax.random.normal(ks[4], (L, DHE), jnp.float32) * s, 'Wq_up_e': jax.random.normal(ks[5], (L, DHE), jnp.float32) * s, 'Wk_up_c': jax.random.normal(ks[6], (L, DHE), jnp.float32) * s, 'Wk_up_e': jax.random.normal(ks[7], (L, DHE), jnp.float32) * s, 'Wv_up': jax.random.normal(ks[8], (L, DH), jnp.float32) * s, 'Wc': jax.random.normal(ks[9], (C, C), jnp.float32) * s}
    _L0_attn_all = _L0_attn_setup()
    _L0_attn_in = {k: v for k, v in _L0_attn_all.items() if k in ('Wq_down', 'Wk_down', 'Wv_down', 'Wq_up_c', 'Wq_up_e', 'Wk_up_c', 'Wk_up_e', 'Wv_up', 'Wc')}
    del _L0_attn_all

    def _L0_ffn_setup():
        import jax, jax.numpy as jnp
        import numpy as np

        def _binarize(w):
            alpha = jax.lax.stop_gradient(jnp.mean(jnp.abs(w), axis=1, keepdims=True))
            bw = alpha * jnp.sign(w)
            return w + jax.lax.stop_gradient(bw - w)
        key = jax.random.key(seed)
        k1, k2, k3, k4, k5 = jax.random.split(key, 5)
        D, H = (256, 1024)
        x = jax.random.normal(k1, (64, 196, D), dtype=jnp.float32)
        w1 = jax.random.normal(k2, (H, D), dtype=jnp.float32) * 0.02
        b1 = jax.random.normal(k3, (H,), dtype=jnp.float32) * 0.02
        w2 = jax.random.normal(k4, (D, H), dtype=jnp.float32) * 0.02
        b2 = jax.random.normal(k5, (D,), dtype=jnp.float32) * 0.02
        return {'x': x, 'w1': w1, 'b1': b1, 'w2': w2, 'b2': b2}
    _L0_ffn_all = _L0_ffn_setup()
    _L0_ffn_in = {k: v for k, v in _L0_ffn_all.items() if k in ('w1', 'b1', 'w2', 'b2')}
    del _L0_ffn_all
    return {'x': x, 'L0_tok_W': _L0_tok_in['W'], 'L0_attn_Wq_down': _L0_attn_in['Wq_down'], 'L0_attn_Wk_down': _L0_attn_in['Wk_down'], 'L0_attn_Wv_down': _L0_attn_in['Wv_down'], 'L0_attn_Wq_up_c': _L0_attn_in['Wq_up_c'], 'L0_attn_Wq_up_e': _L0_attn_in['Wq_up_e'], 'L0_attn_Wk_up_c': _L0_attn_in['Wk_up_c'], 'L0_attn_Wk_up_e': _L0_attn_in['Wk_up_e'], 'L0_attn_Wv_up': _L0_attn_in['Wv_up'], 'L0_attn_Wc': _L0_attn_in['Wc'], 'L0_ffn_w1': _L0_ffn_in['w1'], 'L0_ffn_b1': _L0_ffn_in['b1'], 'L0_ffn_w2': _L0_ffn_in['w2'], 'L0_ffn_b2': _L0_ffn_in['b2']}

def reference(x, L0_tok_W, L0_attn_Wq_down, L0_attn_Wk_down, L0_attn_Wv_down, L0_attn_Wq_up_c, L0_attn_Wq_up_e, L0_attn_Wk_up_c, L0_attn_Wk_up_e, L0_attn_Wv_up, L0_attn_Wc, L0_ffn_w1, L0_ffn_b1, L0_ffn_w2, L0_ffn_b2):
    import jax
    import jax.numpy as jnp

    def _L0_tok_ref(inputs, W):
        import jax, jax.numpy as jnp
        import numpy as np
        from jax import lax
        PATCH = 16
        B, C, H, Wimg = inputs.shape
        patches = lax.conv_general_dilated_patches(inputs, filter_shape=[PATCH, PATCH], window_strides=[PATCH, PATCH], padding='VALID', dimension_numbers=('NCHW', 'HWIO', 'NCHW'))
        patches = patches.reshape(B, -1, C * PATCH * PATCH)
        return jnp.einsum('bnf,fh->bnh', patches, W)

    def _L0_attn_ref(x, Wq_down, Wk_down, Wv_down, Wq_up_c, Wq_up_e, Wk_up_c, Wk_up_e, Wv_up, Wc):
        import jax, jax.numpy as jnp
        import numpy as np
        import math
        B, T, C = (2, 512, 256)
        H, L = (16, 64)
        DH = C // H
        DHE = DH // 2
        THETA = 10000.0

        def _rope_cache(t, dim):
            inv_freq = 1.0 / THETA ** (jnp.arange(0, dim, 2, dtype=jnp.float32) / dim)
            freqs = jnp.arange(t, dtype=jnp.float32)[:, None] * inv_freq[None, :]
            emb = jnp.concatenate((freqs, freqs), axis=-1)
            return (jnp.cos(emb), jnp.sin(emb))

        def _apply_rope(x, cos, sin):
            x1 = x[..., 0::2]
            x2 = x[..., 1::2]
            rot = jnp.stack((-x2, x1), axis=-1).reshape(x.shape)
            return x * cos[None, None] + rot * sin[None, None]
        b, t, c = x.shape
        q_lat = (x @ Wq_down).reshape(b, t, H, L)
        k_lat = (x @ Wk_down).reshape(b, t, H, L)
        v_lat = (x @ Wv_down).reshape(b, t, H, L)
        q_c = jnp.einsum('bthl,ld->bhtd', q_lat, Wq_up_c)
        q_e = jnp.einsum('bthl,ld->bhtd', q_lat, Wq_up_e)
        k_c = jnp.einsum('bthl,ld->bhtd', k_lat, Wk_up_c)
        k_e = jnp.einsum('bthl,ld->bhtd', k_lat, Wk_up_e)
        v = jnp.einsum('bthl,ld->bhtd', v_lat, Wv_up)
        cos, sin = _rope_cache(t, DHE)
        q = jnp.concatenate([q_c, _apply_rope(q_e, cos, sin)], axis=-1)
        k = jnp.concatenate([k_c, _apply_rope(k_e, cos, sin)], axis=-1)
        scale = 1.0 / math.sqrt(DH)
        scores = jnp.einsum('bhqd,bhkd->bhqk', q, k) * scale
        causal = jnp.tril(jnp.ones((t, t), dtype=bool))
        scores = jnp.where(causal[None, None], scores, -jnp.inf)
        att = jax.nn.softmax(scores, axis=-1)
        y = jnp.einsum('bhqk,bhkd->bhqd', att, v)
        y = y.transpose(0, 2, 1, 3).reshape(b, t, c)
        return y @ Wc

    def _L0_ffn_ref(x, w1, b1, w2, b2):
        import jax, jax.numpy as jnp
        import numpy as np

        def _binarize(w):
            alpha = jax.lax.stop_gradient(jnp.mean(jnp.abs(w), axis=1, keepdims=True))
            bw = alpha * jnp.sign(w)
            return w + jax.lax.stop_gradient(bw - w)
        bw1 = _binarize(w1)
        h = jnp.einsum('bsd,hd->bsh', x, bw1) + b1
        h = jax.nn.gelu(h, approximate=False)
        bw2 = _binarize(w2)
        out = jnp.einsum('bsh,dh->bsd', h, bw2) + b2
        return out
    h = _L0_tok_ref(x, L0_tok_W)
    h = h + _L0_attn_ref(_layernorm(h, axis=-1), L0_attn_Wq_down, L0_attn_Wk_down, L0_attn_Wv_down, L0_attn_Wq_up_c, L0_attn_Wq_up_e, L0_attn_Wk_up_c, L0_attn_Wk_up_e, L0_attn_Wv_up, L0_attn_Wc)
    h = h + _L0_ffn_ref(_layernorm(h, axis=-1), L0_ffn_w1, L0_ffn_b1, L0_ffn_w2, L0_ffn_b2)
    return h

_drawn_inputs = setup_inputs


def setup_inputs(seed=0):
    import zlib

    import numpy as np

    out = dict(_drawn_inputs(seed))
    spreads = {}
    factors = {'L0_attn_Wq_down': 8.0,
     'L0_attn_Wk_down': 8.0,
     'L0_attn_Wv_down': 8.0,
     'L0_attn_Wq_up_c': 8.0,
     'L0_attn_Wq_up_e': 8.0,
     'L0_attn_Wk_up_c': 8.0,
     'L0_attn_Wk_up_e': 8.0,
     'L0_attn_Wv_up': 8.0,
     'L0_attn_Wc': 8.0,
     'L0_ffn_b1': 64.0,
     'L0_ffn_b2': 21.166,
     'L0_ffn_w1': 5.98,
     'L0_ffn_w2': 5.106}
    for name, (base, spread) in spreads.items():
        noise = np.random.default_rng([zlib.crc32(name.encode()), seed]).standard_normal(out[name].shape)
        drawn = base * np.exp(spread * noise) if base else spread * noise
        out[name] = jnp.asarray(drawn.astype(out[name].dtype))
    for name, factor in factors.items():
        out[name] = (out[name] * factor).astype(out[name].dtype)
    return out
```

```python
import math

import numpy as np

import concourse.bass as bass
from concourse import mybir
from contextlib import ExitStack

FP32 = mybir.dt.float32
FP32R = mybir.dt.float32r
BF16 = mybir.dt.bfloat16
ALU = mybir.AluOpType
ACT = mybir.ActivationFunctionType
AX = mybir.AxisListType

IMAGES, CHANNELS, SIDE, PATCH = 64, 3, 224, 16
T = (SIDE // PATCH) ** 2
F = CHANNELS * PATCH * PATCH
D = 256
HEADS, LATENT, DH = 16, 64, 16
DR = DH // 2
HID = 1024
THETA, EPS = 10000.0, 1e-5

P = 128
PER = 2
CHUNKS = IMAGES // PER
N = PER * T
Q = T // 2
TILES = N // Q
KF, KD, KH = F // P, D // P, HID // P
KEYS = (P, T - P)
COMBOS = ((0, 0), (1, 0), (2, 0), (0, 1), (1, 1), (0, 2))
ROWS = len(COMBOS) * DH
GUARD = 3
QUADS = HEADS // 4
MASKED = -1e30


def vit_layer(nc, x_in, tok_in, down_in, up_in, wc_in, w1t_in, w1_in, b1_in, w2t_in, b2_in,
              cos_in, sin_in, mask_in, ident_in, y_out):
    with ExitStack() as ctx:
        def sb(name, shape, dt=FP32):
            return ctx.enter_context(nc.sbuf_tensor(name, shape, dt))

        tok_hi, tok_lo = sb("tok_hi", [P, KF, D], FP32R), sb("tok_lo", [P, KF, D], FP32R)
        wqk_hi, wqk_lo = sb("wqk_hi", [P, KD, 2 * D], FP32R), sb("wqk_lo", [P, KD, 2 * D], FP32R)
        wv_hi, wv_lo = sb("wv_hi", [P, KD, D], FP32R), sb("wv_lo", [P, KD, D], FP32R)
        wc_hi, wc_lo = sb("wc_hi", [P, KD, D], FP32R), sb("wc_lo", [P, KD, D], FP32R)
        sign1 = sb("sign1", [P, KD, HID], FP32R)
        sign2 = sb("sign2", [P, KH, D], FP32R)
        alpha1, b1 = sb("alpha1", [P, KH]), sb("b1", [P, KH])
        alpha2, b2 = sb("alpha2", [Q, D]), sb("b2", [Q, D])
        cos, sin = sb("cos", [P, N]), sb("sin", [P, N])
        ident = sb("ident", [Q, Q])
        ident_bf, mask_bf = sb("ident_bf", [Q, Q], BF16), sb("mask_bf", [Q, 4 * Q], BF16)
        minus_half = sb("minus_half", [Q, TILES])

        prepare_weights(nc, locals())
        run_chunks(nc, ctx, sb, locals())


def prepare_weights(nc, w):
    with ExitStack() as ctx:
        def sb(name, shape, dt=FP32):
            return ctx.enter_context(nc.sbuf_tensor(name, shape, dt))

        def sem(name):
            return ctx.enter_context(nc.semaphore(name))

        tok = sb("tok_raw", [P, KF, D])
        down = [sb(f"down_{s}", [LATENT, HEADS, D]) for s in "qkv"]
        up = sb("up", [LATENT, 3, DH])
        wc = sb("wc_raw", [P, KD, D])
        w1t, w1, w2t = sb("w1t", [P, KD * HID]), sb("w1", [P, KH, D]), sb("w2t", [P, KH * D])
        negative1, negative2 = sb("negative1", [P, KD * HID]), sb("negative2", [P, KH * D])
        abs2 = sb("abs2", [P, KH, D])
        ones = sb("ones", [P, Q])
        mask = sb("mask", [Q, 4 * Q])
        folded = [ctx.enter_context(nc.psum_tensor(f"folded{i}", [P, 512], FP32)) for i in range(6)]
        mean2 = ctx.enter_context(nc.psum_tensor("mean2", [Q, D], FP32))

        loads = [(tok, w["tok_in"]), (w1t, w["w1t_in"]), (w1, w["w1_in"]), (w2t, w["w2t_in"]),
                 (wc, w["wc_in"]), (w["b1"], w["b1_in"]), (w["b2"], w["b2_in"]), (w["cos"], w["cos_in"]),
                 (w["sin"], w["sin_in"]), (mask, w["mask_in"]), (w["ident"], w["ident_in"])]
        weights_loaded, latent_loaded = sem("weights_loaded"), sem("latent_loaded")
        fold_done, ones_set, abs_done, mean_done = sem("fold_done"), sem("ones_set"), sem("abs_done"), sem("mean_done")
        hi_done, negative_done, sum_done, prep_done = sem("hi_done"), sem("negative_done"), sem("sum_done"), sem("prep_done")
        block = ctx.enter_context(nc.Block())

        @block.sync
        def _(sp):
            for s in range(3):
                sp.dma_start(down[s][:, :, :], w["down_in"][s]).then_inc(latent_loaded, 16)
            sp.dma_start(up[:, :, :], w["up_in"]).then_inc(latent_loaded, 16)
            for to, of in loads:
                sp.dma_start(to[tuple(slice(None) for _ in to.shape)], of).then_inc(weights_loaded, 16)

        @block.tensor
        def _(pe):
            pe.wait_ge(latent_loaded, 4 * 16)
            for s in range(3):
                for k in range(KD):
                    for h in range(HEADS):
                        bank = folded[2 * s + k]
                        out = bank[:, h:D:HEADS] if s < 2 else bank[:, h * DH:(h + 1) * DH]
                        mm = pe.matmul(out, down[s][:, h, k * P:(k + 1) * P], up[:, s, :], start=True, stop=True)
                    mm.then_inc(fold_done, 1)
            pe.wait_ge(ones_set, 1)
            pe.wait_ge(abs_done, 1)
            for k in range(KH):
                mm = pe.matmul(mean2[:, :], ones[:, :], abs2[:, k, :], start=(k == 0), stop=(k == KH - 1))
            mm.then_inc(mean_done, 1)

        @block.vector
        def _(dve):
            dve.memset(ones[:, :], 1.0).then_inc(ones_set, 1)
            dve.memset(w["minus_half"][:, :], -0.5)
            dve.wait_ge(weights_loaded, len(loads) * 16)
            dve.scalar_tensor_tensor(out=abs2[:, :, :].rearrange("p k d -> p (k d)"), in0=w2t[:, :], scalar=-1.0,
                                     in1=w2t[:, :], op0=ALU.mult, op1=ALU.max).then_inc(abs_done, 1)
            for n, (negative, raw) in enumerate(((negative1, w1t), (negative2, w2t))):
                dve.tensor_scalar(negative[:, :], raw[:, :], 0.0, None, ALU.is_lt).then_inc(negative_done, 1)
            for n, (negative, raw, out) in enumerate(((negative1, w1t, w["sign1"]), (negative2, w2t, w["sign2"]))):
                dve.wait_ge(negative_done, n + 1)
                dve.scalar_tensor_tensor(out=out[:, :, :].rearrange("p k d -> p (k d)"), in0=raw[:, :], scalar=0.0,
                                         in1=negative[:, :], op0=ALU.is_gt, op1=ALU.subtract).then_inc(prep_done, 1)
            dve.tensor_reduce(w["alpha1"][:, :], w1[:, :, :], AX.X, ALU.add,
                              apply_absolute_value=True).then_inc(sum_done, 1)
            dve.tensor_copy(w["ident_bf"][:, :], w["ident"][:, :]).then_inc(prep_done, 1)
            dve.tensor_copy(w["mask_bf"][:, :], mask[:, :]).then_inc(prep_done, 1)
            dve.wait_ge(sum_done, 1)
            dve.tensor_scalar(w["alpha1"][:, :], w["alpha1"][:, :], 1.0 / D, None, ALU.mult).then_inc(prep_done, 1)
            dve.tensor_copy(w["tok_hi"][:, :, :], tok[:, :, :]).then_inc(hi_done, 1)
            dve.tensor_copy(w["wc_hi"][:, :, :], wc[:, :, :]).then_inc(hi_done, 1)
            dve.wait_ge(hi_done, 1)
            dve.tensor_tensor(w["tok_lo"][:, :, :], tok[:, :, :], w["tok_hi"][:, :, :].bitcast(FP32),
                              ALU.subtract).then_inc(prep_done, 1)
            dve.wait_ge(hi_done, 2)
            dve.tensor_tensor(w["wc_lo"][:, :, :], wc[:, :, :], w["wc_hi"][:, :, :].bitcast(FP32),
                              ALU.subtract).then_inc(prep_done, 1)
            parts = []
            for s in range(3):
                for k in range(KD):
                    at = slice(s * D, (s + 1) * D) if s < 2 else slice(0, D)
                    parts.append((folded[2 * s + k][:, 0:D], DH ** -0.5 if s == 0 else 1.0,
                                  (w["wqk_hi"] if s < 2 else w["wv_hi"])[:, k, at],
                                  (w["wqk_lo"] if s < 2 else w["wv_lo"])[:, k, at]))
            for n, (psum, scale, hi, lo) in enumerate(parts):
                dve.wait_ge(fold_done, n + 1)
                dve.tensor_scalar(hi, psum, scale, None, ALU.mult).then_inc(hi_done, 1)
                dve.wait_ge(hi_done, n + 3)
                dve.scalar_tensor_tensor(out=lo, in0=psum, scalar=scale, in1=hi.bitcast(FP32),
                                         op0=ALU.mult, op1=ALU.subtract).then_inc(prep_done, 1)
            dve.wait_ge(mean_done, 1)
            dve.tensor_scalar(w["alpha2"][:, :], mean2[:, :], 1.0 / HID, None, ALU.mult).then_inc(prep_done, 1)
            dve.wait_ge(prep_done, 2 + 3 + 2 + len(parts) + 1)


class Event:

    def __init__(self, ctx, nc, name, per):
        self.sem, self.per = ctx.enter_context(nc.semaphore(name)), per

    def count(self, chunk, k):
        return chunk * self.per + k

    def all(self, chunk):
        return (chunk + 1) * self.per


def there(chunk):
    return not isinstance(chunk, int) or chunk >= 0


def known(eng, value):
    return value if isinstance(value, int) else eng.to_reg(value)


def run_chunks(nc, ctx, sb, w):
    DMA = 16

    def event(name, per):
        return Event(ctx, nc, name, per)

    x_raw = sb("x_raw", [P, KF, N])
    x_hi, x_lo = sb("x_hi", [P, KF, N], FP32R), sb("x_lo", [P, KF, N], FP32R)
    h_new, h_old = sb("h_new", [Q, TILES, D]), sb("h_old", [Q, TILES, D])
    stats = [sb(f"stats{i}", [Q, TILES, 6]) for i in range(2)]
    moments = [sb(f"moments{i}", [Q, TILES, 2]) for i in range(2)]
    shifted = [sb(f"shifted{i}", [Q, TILES]) for i in range(2)]
    rstd = [sb(f"rstd{i}", [Q, TILES]) for i in range(2)]
    xn = [sb(f"xn{i}", [Q, TILES, D]) for i in range(2)]
    xn_hi = [sb(f"xn_hi{i}", [P, KD, N], FP32R) for i in range(2)]
    xn_lo = [sb(f"xn_lo{i}", [P, KD, N], FP32R) for i in range(2)]
    qk = sb("qk", [P, 4, N])
    turned = sb("turned", [P, 2, N])
    part = [sb(f"part{i}", [P, 4, N], BF16) for i in range(3)]
    q_stack = sb("q_stack", [ROWS + GUARD, HEADS, N], BF16)
    k_stack = sb("k_stack", [ROWS + GUARD, HEADS, N], BF16)
    negmax = sb("negmax", [Q, HEADS, TILES])
    guard = sb("guard", [HEADS * TILES, GUARD, Q], BF16)
    guard_rest = sb("guard_rest", [HEADS * TILES, Q])
    e_far = sb("e_far", [P, 2, 4, T])
    e_near = sb("e_near", [P, 2, 4, KEYS[1]])
    values = sb("values", [P, PER, 2, HEADS, 2 * DH])
    o_sums = sb("o_sums", [P, QUADS, N])
    y, den = sb("y", [P, KD, N]), sb("den", [P, KD, N])
    y_hi, y_lo = sb("y_hi", [P, KD, N], FP32R), sb("y_lo", [P, KD, N], FP32R)
    h1 = sb("h1", [Q, TILES, D])
    g = sb("g", [P, 2, N])
    g_hi, g_lo = sb("g_hi", [P, KH, N], FP32R), sb("g_lo", [P, KH, N], FP32R)
    out = sb("out_sb", [Q, TILES, D])

    def bank(name):
        return ctx.enter_context(nc.psum_tensor(name, [P, 512], FP32))

    dense = [bank("dense0"), bank("dense1")]
    score = [bank("score0"), bank("score1")]
    far = [bank("far0"), bank("far1")]
    near = bank("near")
    value_bank = bank("value_bank")
    value_banks = [value_bank, score[0]]

    x_loaded = event("x_loaded", DMA)
    x_hi_done, x_lo_done = event("x_hi_done", 2), event("x_lo_done", 2)
    tok_done, h_ready, h_moved = event("tok_done", 2), event("h_ready", 2), event("h_moved", 1)
    stats_done = [event(f"stats_done{i}", TILES) for i in range(2)]
    moments_done = [event(f"moments_done{i}", TILES) for i in range(2)]
    shifted_done = [event(f"shifted_done{i}", 1) for i in range(2)]
    rstd_done = [event(f"rstd_done{i}", 1) for i in range(2)]
    xn_done = [event(f"xn_done{i}", 1) for i in range(2)]
    turn_done = [event(f"turn_done{i}", KD) for i in range(2)]
    xn_hi_done = [event(f"xn_hi_done{i}", KD) for i in range(2)]
    xn_lo_done = [event(f"xn_lo_done{i}", KD) for i in range(2)]
    qk_mm_done, qk_ready = event("qk_mm_done", 4), event("qk_ready", 4)
    swapped_done, cos_done, sin_done, rope_done = (event("swapped_done", 2), event("cos_done", 2),
                                                   event("sin_done", 2), event("rope_done", 2))
    part0_done, rest_done, part1_done, part2_done = (event("part0_done", 2), event("rest_done", 2),
                                                     event("part1_done", 2), event("part2_done", 2))
    stack_loaded = event("stack_loaded", 4 * len(COMBOS) * DMA)
    v_mm_done, v_ready = event("v_mm_done", PER), event("v_ready", PER * 2)
    FILLS = PER * (4 + 8)
    fill_done, max_done = event("fill_done", FILLS), event("max_done", FILLS)
    max_turned, guard_split, guard_rest_done, guard_loaded = (event("max_turned", 1), event("guard_split", 3),
                                                              event("guard_rest_done", 2), event("guard_loaded", GUARD * DMA))
    G = QUADS * PER
    far_done, near_done = event("far_done", 2 * G), event("near_done", G)
    exp_far, exp_near = event("exp_far", 2 * G), event("exp_near", G)
    masked_done, pv_done, o_ready = event("masked_done", 2 * G), event("pv_done", G), event("o_ready", QUADS)
    y_loaded = event("y_loaded", 16 * DMA)
    recip_done, y_done, y_hi_done, y_lo_done = (event("recip_done", 1), event("y_done", 1),
                                                event("y_hi_done", 1), event("y_lo_done", KD))
    proj_done, h1_ready, h1_biased = event("proj_done", 2), event("h1_ready", 2), event("h1_biased", 1)
    up_done, gelu_done, g_hi_done, g_lo_even, g_lo_odd = (event("up_done", KH), event("gelu_done", KH),
                                                          event("g_hi_done", KH), event("g_lo_even", KH // 2),
                                                          event("g_lo_odd", KH // 2))
    down_done, scaled_done, out_ready, out_stored = (event("down_done", 2), event("scaled_done", 2),
                                                     event("out_ready", 2), event("out_stored", DMA))
    const_done = event("const_done", 1)
    CONSTS = 5

    def seen(x):
        return x.bitcast(FP32)


    block = ctx.enter_context(nc.Block())

    @block.sync
    def _(sp):
        def load_x(m, prev):
            src = w["x_in"][m] if isinstance(m, int) else w["x_in"][bass.ds(sp.snap(m), 1)].rearrange("a p k n -> (a p) k n")
            value0 = known(sp, x_hi_done.all(prev)) if there(prev) else 0
            value1 = known(sp, x_lo_done.all(prev)) if there(prev) else 0
            sp.wait_ge(const_done.sem, CONSTS)
            if there(prev):
                sp.wait_ge(x_hi_done.sem, value0)
            if there(prev):
                sp.wait_ge(x_lo_done.sem, value1)
            sp.dma_start(x_raw[:, :, :], src).then_inc(x_loaded.sem, 16)

        def load_guard(c):
            for r in range(GUARD):
                value = known(sp, guard_split.count(c, r + 1))
                sp.wait_ge(const_done.sem, CONSTS)
                sp.wait_ge(guard_split.sem, value)
                sp.dma_start(q_stack[ROWS + r:ROWS + r + 1, :, :], guard[:, r, :]).then_inc(guard_loaded.sem, 16)

        def load_y(c):
            value0 = known(sp, y_hi_done.all(c - 1)) if there(c - 1) else 0
            value1 = known(sp, y_lo_done.all(c - 1)) if there(c - 1) else 0
            value2 = known(sp, o_ready.all(c))
            sp.wait_ge(const_done.sem, CONSTS)
            if there(c - 1):
                sp.wait_ge(y_hi_done.sem, value0)
            if there(c - 1):
                sp.wait_ge(y_lo_done.sem, value1)
            sp.wait_ge(o_ready.sem, value2)
            for odd in range(2):
                for j in range(4):
                    rows = slice(odd * 64 + j * DH, odd * 64 + (j + 1) * DH)
                    sp.dma_start(den[rows, :, :], o_sums[32 * j + DH:32 * j + 2 * DH, odd:QUADS:2, :]).then_inc(y_loaded.sem, 16)
                    sp.dma_start(y[rows, :, :], o_sums[32 * j:32 * j + DH, odd:QUADS:2, :]).then_inc(y_loaded.sem, 16)

        def load_stack(n, c):
            value0 = known(sp, far_done.all(c)) if there(c) else 0
            value1 = known(sp, near_done.all(c)) if there(c) else 0
            sp.wait_ge(const_done.sem, CONSTS)
            if there(c):
                sp.wait_ge(far_done.sem, value0)
            if there(c):
                sp.wait_ge(near_done.sem, value1)
            for i, made in enumerate((part0_done, part1_done, part2_done)):
                value = known(sp, made.all(n))
                sp.wait_ge(const_done.sem, CONSTS)
                sp.wait_ge(made.sem, value)
                for r, (of_q, of_k) in enumerate(COMBOS):
                    for side, stack, of in ((0, q_stack, of_q), (1, k_stack, of_k)):
                        if of != i:
                            continue
                        for rotary in range(2):
                            row = r * DH + rotary * DR
                            sp.dma_start(stack[row:row + DR, :, :], part[i][:, 2 * side + rotary, :]).then_inc(stack_loaded.sem, 16)

        def store(b):
            dst = (w["y_out"][b] if isinstance(b, int) else w["y_out"][bass.ds(sp.snap(b), 1)].rearrange("a t p d -> (a t) p d"))
            value = known(sp, out_ready.all(b))
            sp.wait_ge(const_done.sem, CONSTS)
            sp.wait_ge(out_ready.sem, value)
            sp.dma_start(dst.rearrange("t p d -> p t d"), out[:, :, :]).then_inc(out_stored.sem, 16)

        def body(c, attend=True, front=True, ffn=True, prefetch=True):
            if prefetch:
                load_x(c + 2, c + 1)
            if attend:
                load_guard(c)
                load_y(c)
            if front:
                load_stack(c + 1, c)
            if ffn:
                store(c - 1)

        load_x(0, -1)
        load_x(1, 0)
        load_stack(0, -1)
        body(0, ffn=False)
        body(1)
        with sp.Fori(2, CHUNKS - 2) as c:
            body(c)
        body(CHUNKS - 2, prefetch=False)
        body(CHUNKS - 1, prefetch=False, front=False)
        body(CHUNKS, prefetch=False, front=False, attend=False)
        sp.wait_ge(out_stored.sem, out_stored.all(CHUNKS - 1))

    @block.tensor
    def _(pe):
        def tokens(n, piece):
            t, half = divmod(piece, 2)
            u = t // 2
            if piece == 0:
                pe.wait_ge(x_hi_done.sem, x_hi_done.all(n))
                pe.wait_ge(x_lo_done.sem, x_lo_done.all(n))
            steps = [(k, a, b) for k in range(KF) for a, b in ((x_hi, w["tok_hi"]), (x_lo, w["tok_hi"]), (x_hi, w["tok_lo"]))]
            for i in range(9 * half, 9 * half + 9):
                k, a, b = steps[i]
                mm = pe.matmul(dense[u][0:Q, (t % 2) * D:(t % 2 + 1) * D], a[:, k, t * Q:(t + 1) * Q], b[:, k, :],
                               start=(i == 0), stop=(i == len(steps) - 1))
            if piece % 4 == 3:
                mm.then_inc(tok_done.sem, 1)

        def turn_ffn(b, front):
            pe.wait_ge(xn_done[1].sem, xn_done[1].all(b))
            for k in range(KD):
                if front:
                    pe.wait_ge(h_ready.sem, h_ready.count(b + 2, k + 1))
                else:
                    pe.wait_ge(h1_ready.sem, h1_ready.count(b, k + 1))
                for t in range(TILES):
                    mm = pe.transpose(dense[k][:, t * Q:(t + 1) * Q], xn[1][:, t, k * P:(k + 1) * P], w["ident"][:, :])
                mm.then_inc(turn_done[1].sem, 1)

        def turn_front(n, ffn):
            pe.wait_ge(xn_done[0].sem, xn_done[0].all(n))
            for k in range(KD):
                if ffn:
                    pe.wait_ge(xn_lo_done[1].sem, xn_lo_done[1].count(n - 2, k + 1))
                else:
                    pe.wait_ge(h_ready.sem, h_ready.count(n, k + 1))
                for t in range(TILES):
                    mm = pe.transpose(dense[k][:, t * Q:(t + 1) * Q], xn[0][:, t, k * P:(k + 1) * P], w["ident"][:, :])
                mm.then_inc(turn_done[0].sem, 1)

        def project_qk(n, m):
            if m == 0:
                pe.wait_ge(xn_hi_done[0].sem, xn_hi_done[0].all(n))
                pe.wait_ge(xn_lo_done[0].sem, xn_lo_done[0].all(n))
            if m >= 2:
                pe.wait_ge(qk_ready.sem, qk_ready.count(n, m - 1))
            steps = [(k, a, b) for k in range(KD) for a, b in ((w["wqk_hi"], xn_hi[0]), (w["wqk_lo"], xn_hi[0]), (w["wqk_hi"], xn_lo[0]))]
            for i, (k, a, b) in enumerate(steps):
                mm = pe.matmul(dense[m % 2][:, 0:N], a[:, k, m * P:(m + 1) * P], b[:, k, :],
                               start=(i == 0), stop=(i == len(steps) - 1))
            mm.then_inc(qk_mm_done.sem, 1)

        def project_v(n, image):
            pe.wait_ge(qk_ready.sem, qk_ready.count(n, image + 3))
            steps = [(k, a, b) for k in range(KD) for a, b in ((xn_hi[0], w["wv_hi"]), (xn_lo[0], w["wv_hi"]), (xn_hi[0], w["wv_lo"]))]
            for kt, keys in enumerate(KEYS):
                at = image * T + kt * P
                for i, (k, a, b) in enumerate(steps):
                    mm = pe.matmul(dense[image][0:keys, kt * D:(kt + 1) * D], a[:, k, at:at + keys], b[:, k, :],
                                   start=(i == 0), stop=(i == len(steps) - 1))
            mm.then_inc(v_mm_done.sem, 1)

        def scores(c, f):
            image, r = divmod(f, 12)
            if f == 0:
                pe.wait_ge(stack_loaded.sem, stack_loaded.all(c))
                if there(c - 1):
                    pe.wait_ge(o_ready.sem, o_ready.all(c - 1))
            if f >= 2:
                pe.wait_ge(max_done.sem, max_done.count(c, f - 1))
            else:
                if there(c - 1):
                    pe.wait_ge(max_done.sem, max_done.all(c - 1))
            if r < 4:
                qt, heads = 0, range(4 * r, 4 * r + 4)
            else:
                qt, heads = 1, range(2 * (r - 4), 2 * (r - 4) + 2)
            keys = Q * (qt + 1)
            bank = score[f % 2][0:Q, 0:len(heads) * keys]
            diagonal = bank.rearrange("q (h k) -> q h k", h=len(heads))[:, :, keys - Q:keys]
            pe.matmul(diagonal, w["ident_bf"][:, :], w["mask_bf"][:, 0:len(heads) * Q].rearrange("q (h k) -> q h k", h=len(heads)),
                      start=True, stop=False, skip_group_check=True)
            at = image * T
            for i, h in enumerate(heads):
                mm = pe.matmul(bank[:, i * keys:(i + 1) * keys], q_stack[0:ROWS, h, at + qt * Q:at + (qt + 1) * Q],
                               k_stack[0:ROWS, h, at:at + keys], start=False, stop=(i == len(heads) - 1),
                               skip_group_check=True)
            mm.then_inc(fill_done.sem, 1)

        def turn_max(c):
            value0 = known(pe, max_done.all(c))
            value1 = known(pe, o_ready.all(c - 1)) if there(c - 1) else 0
            pe.wait_ge(const_done.sem, CONSTS)
            pe.wait_ge(max_done.sem, value0)
            if there(c - 1):
                pe.wait_ge(o_ready.sem, value1)
            pe.transpose(value_bank[0:HEADS * TILES, 0:Q], negmax[:, :, :].rearrange("q h t -> q (h t)"),
                         w["ident"][:, :]).then_inc(max_turned.sem, 1)

        def scores_t(c, i):
            quad, image = divmod(i, PER)
            at = image * T
            if i == 0:
                pe.wait_ge(guard_loaded.sem, guard_loaded.all(c))
            for pair in range(2):
                if i > 0:
                    pe.wait_ge(exp_far.sem, exp_far.count(c, 2 * i + pair - 1))
                else:
                    if there(c - 1):
                        pe.wait_ge(exp_far.sem, exp_far.all(c - 1))
                for j in range(2):
                    h = 4 * quad + 2 * pair + j
                    mm = pe.matmul(far[pair][:, j * T:(j + 1) * T], k_stack[:, h, at:at + P], q_stack[:, h, at:at + T],
                                   start=True, stop=True)
                mm.then_inc(far_done.sem, 1)
            if i > 0:
                pe.wait_ge(exp_near.sem, exp_near.count(c, i))
            else:
                if there(c - 1):
                    pe.wait_ge(exp_near.sem, exp_near.all(c - 1))
            for j in range(4):
                h = 4 * quad + j
                mm = pe.matmul(near[0:KEYS[1], j * KEYS[1]:(j + 1) * KEYS[1]], k_stack[:, h, at + P:at + T],
                               q_stack[:, h, at + P:at + T], start=True, stop=True)
            mm.then_inc(near_done.sem, 1)

        def weigh(c, i):
            quad, image = divmod(i, PER)
            bank = value_banks[quad % 2]
            if i == 0:
                pe.wait_ge(v_ready.sem, v_ready.all(c))
                pe.wait_ge(guard_rest_done.sem, guard_rest_done.all(c))
            if quad >= 2:
                pe.wait_ge(o_ready.sem, o_ready.count(c, quad - 1))
            pe.wait_ge(masked_done.sem, masked_done.count(c, 2 * i + 2))
            for j in range(4):
                pe.matmul(bank[32 * j:32 * j + 32, image * T:(image + 1) * T], values[:, image, 0, 4 * quad + j, :],
                          e_far[:, i % 2, j, :], start=True, stop=False, skip_group_check=True)
            for j in range(4):
                mm = pe.matmul(bank[32 * j:32 * j + 32, image * T + P:(image + 1) * T], values[:, image, 1, 4 * quad + j, :],
                               e_near[:, i % 2, j, :], start=False, stop=True, skip_group_check=True)
            mm.then_inc(pv_done.sem, 1)

        def project_out(b, u):
            if u == 0:
                if there(b - 1):
                    pe.wait_ge(scaled_done.sem, scaled_done.all(b - 1))
                pe.wait_ge(v_ready.sem, v_ready.all(min(b + 1, CHUNKS - 1) if isinstance(b, int) else b + 1))
                pe.wait_ge(y_hi_done.sem, y_hi_done.all(b))
                pe.wait_ge(y_lo_done.sem, y_lo_done.all(b))
            steps = [(k, a, v) for k in range(KD) for a, v in ((y_hi, w["wc_hi"]), (y_lo, w["wc_hi"]), (y_hi, w["wc_lo"]))]
            for t in (2 * u, 2 * u + 1):
                for i, (k, a, v) in enumerate(steps):
                    mm = pe.matmul(dense[u][0:Q, (t % 2) * D:(t % 2 + 1) * D], a[:, k, t * Q:(t + 1) * Q], v[:, k, :],
                                   start=(i == 0), stop=(i == len(steps) - 1))
            mm.then_inc(proj_done.sem, 1)

        def ffn_up(b, m, front):
            if m >= 2:
                pe.wait_ge(gelu_done.sem, gelu_done.count(b, m - 1))
            elif front:
                pe.wait_ge(v_ready.sem, v_ready.count(b + 2, 2 * (m + 1)))
            if m == 0:
                pe.wait_ge(xn_hi_done[1].sem, xn_hi_done[1].all(b))
                pe.wait_ge(xn_lo_done[1].sem, xn_lo_done[1].all(b))
            steps = [(k, v) for k in range(KD) for v in (xn_hi[1], xn_lo[1])]
            for i, (k, v) in enumerate(steps):
                mm = pe.matmul(dense[m % 2][:, 0:N], w["sign1"][:, k, m * P:(m + 1) * P], v[:, k, :],
                               start=(i == 0), stop=(i == len(steps) - 1))
            mm.then_inc(up_done.sem, 1)

        def ffn_down(b, u):
            pe.wait_ge(gelu_done.sem, gelu_done.count(b, KH - 1 + u))
            for t in (2 * u, 2 * u + 1):
                for m in range(KH):
                    if t == 0:
                        pe.wait_ge(g_hi_done.sem, g_hi_done.count(b, m + 1))
                        lo = g_lo_odd if m % 2 else g_lo_even
                        pe.wait_ge(lo.sem, lo.count(b, m // 2 + 1))
                    for a in (g_hi, g_lo):
                        mm = pe.matmul(dense[u][0:Q, (t % 2) * D:(t % 2 + 1) * D], a[:, m, t * Q:(t + 1) * Q], w["sign2"][:, m, :],
                                       start=(m == 0 and a is g_hi), stop=(m == KH - 1 and a is g_lo))
            mm.then_inc(down_done.sem, 1)

        def body(c, attend=True, front=True, ffn=True, prefetch=True):
            n, b = c + 1, c - 1
            if ffn:
                project_out(b, 0)
                project_out(b, 1)
            piece = 0
            if attend:
                for f in range(FILLS):
                    scores(c, f)
                    if front and f % 2 and piece < 8:
                        if piece % 4 == 0:
                            if ffn:
                                pe.wait_ge(h1_ready.sem, h1_ready.count(b, piece // 4 + 1))
                            else:
                                pe.wait_ge(v_ready.sem, v_ready.count(c, 2 * (piece // 4 + 1)))
                        tokens(n, piece)
                        piece += 1
                turn_max(c)
            if ffn:
                turn_ffn(b, front)
            if front:
                turn_front(n, ffn)
                project_qk(n, 0)
                project_qk(n, 1)
            if attend:
                for i in range(G):
                    scores_t(c, i)
                    if front and i == 1:
                        project_qk(n, 2)
                    if front and i == 3:
                        project_qk(n, 3)
                    if front and i == 5:
                        project_v(n, 0)
                    if front and i == 7:
                        project_v(n, 1)
                    if i >= 2:
                        weigh(c, i - 2)
                weigh(c, G - 2)
                weigh(c, G - 1)
            if ffn:
                for m in range(KH):
                    ffn_up(b, m, front)
                ffn_down(b, 0)
                ffn_down(b, 1)

        pe.wait_ge(const_done.sem, const_done.count(0, CONSTS))
        for piece in range(8):
            tokens(0, piece)
        turn_front(0, False)
        for m in range(4):
            project_qk(0, m)
        for image in range(PER):
            project_v(0, image)
        body(0, ffn=False)
        body(1)
        with pe.Fori(2, CHUNKS - 2) as c:
            body(c)
        body(CHUNKS - 2, prefetch=False)
        body(CHUNKS - 1, prefetch=False, front=False)
        body(CHUNKS, prefetch=False, front=False, attend=False)

    @block.scalar
    def _(act):
        def split_x(m):
            act.wait_ge(x_loaded.sem, x_loaded.all(m))
            if there(m - 1):
                act.wait_ge(tok_done.sem, tok_done.all(m - 1))
            for half in range(2):
                at = slice(half * KF // 2, (half + 1) * KF // 2)
                act.copy(x_hi[:, at, :], x_raw[:, at, :]).then_inc(x_hi_done.sem, 1)

        def keep_h(n, u):
            act.wait_ge(tok_done.sem, tok_done.count(n, u + 1))
            if u == 0:
                if there(n - 1):
                    act.wait_ge(h_moved.sem, h_moved.all(n - 1))
            act.copy(h_new[:, 2 * u:2 * u + 2, :].rearrange("q t d -> q (t d)"), dense[u][0:Q, 0:2 * D]).then_inc(h_ready.sem, 1)

        def split_turned(i, n):
            if i == 0:
                if there(n - 1):
                    act.wait_ge(qk_mm_done.sem, qk_mm_done.all(n - 1))
                if there(n - 1):
                    act.wait_ge(v_mm_done.sem, v_mm_done.all(n - 1))
            else:
                if there(n - 1):
                    act.wait_ge(up_done.sem, up_done.all(n - 1))
            for k in range(KD):
                act.wait_ge(turn_done[i].sem, turn_done[i].count(n, k + 1))
                act.copy(xn_hi[i][:, k, :], dense[k][:, 0:N]).then_inc(xn_hi_done[i].sem, 1)

        def keep_qk(n, m):
            act.wait_ge(qk_mm_done.sem, qk_mm_done.count(n, m + 1))
            if m == 0:
                if there(n - 1):
                    act.wait_ge(part2_done.sem, part2_done.all(n - 1))
            act.copy(qk[:, m, :], dense[m % 2][:, 0:N]).then_inc(qk_ready.sem, 1)

        def keep_v(n, image):
            act.wait_ge(v_mm_done.sem, v_mm_done.count(n, image + 1))
            if there(n - 1):
                act.wait_ge(pv_done.sem, pv_done.all(n - 1))
            for kt, keys in enumerate(KEYS):
                act.copy(values[0:keys, image, kt, :, 0:DH],
                         dense[image][0:keys, kt * D:(kt + 1) * D].rearrange("k (h d) -> k h d", h=HEADS)).then_inc(v_ready.sem, 1)

        def exps(c, i):
            if i >= 2:
                act.wait_ge(pv_done.sem, pv_done.count(c, i - 1))
            else:
                if there(c - 1):
                    act.wait_ge(pv_done.sem, pv_done.all(c - 1))
            for pair in range(2):
                act.wait_ge(far_done.sem, far_done.count(c, 2 * i + pair + 1))
                act.activation(e_far[:, i % 2, 2 * pair:2 * pair + 2, :].rearrange("k h q -> k (h q)"), far[pair][:, 0:2 * T],
                               ACT.Exp).then_inc(exp_far.sem, 1)
            act.wait_ge(near_done.sem, near_done.count(c, i + 1))
            act.activation(e_near[0:KEYS[1], i % 2, :, :].rearrange("k h q -> k (h q)"), near[0:KEYS[1], 0:4 * KEYS[1]],
                           ACT.Exp).then_inc(exp_near.sem, 1)

        def gelus(b):
            for m in range(KH):
                act.wait_ge(up_done.sem, up_done.count(b, m + 1))
                if m >= 2:
                    act.wait_ge(g_hi_done.sem, g_hi_done.count(b, m - 1))
                    lo = g_lo_odd if m % 2 else g_lo_even
                    act.wait_ge(lo.sem, lo.count(b, m // 2))
                else:
                    if there(b - 1):
                        act.wait_ge(g_hi_done.sem, g_hi_done.all(b - 1))
                    lo = g_lo_odd if m % 2 else g_lo_even
                    if there(b - 1):
                        act.wait_ge(lo.sem, lo.all(b - 1))
                act.activation(g[:, m % 2, :], dense[m % 2][:, 0:N], ACT.Gelu, bias=w["b1"][:, m:m + 1],
                               scale=w["alpha1"][:, m:m + 1]).then_inc(gelu_done.sem, 1)

        def split_y(c):
            act.wait_ge(y_done.sem, y_done.all(c))
            if there(c - 1):
                act.wait_ge(proj_done.sem, proj_done.all(c - 1))
            act.copy(y_hi[:, :, :], y[:, :, :]).then_inc(y_hi_done.sem, 1)

        def body(c, attend=True, front=True, ffn=True, prefetch=True):
            n, b = c + 1, c - 1
            if front:
                keep_h(n, 0)
                keep_h(n, 1)
            if ffn:
                split_turned(1, b)
            if front:
                split_turned(0, n)
                keep_qk(n, 0)
                keep_qk(n, 1)
            if prefetch:
                split_x(c + 2)
            if attend:
                for i in range(G):
                    exps(c, i)
                    if front and i == 1:
                        keep_qk(n, 2)
                    if front and i == 3:
                        keep_qk(n, 3)
            if front:
                keep_v(n, 0)
                keep_v(n, 1)
            if ffn:
                gelus(b)
            if attend:
                split_y(c)

        split_x(0)
        keep_h(0, 0)
        keep_h(0, 1)
        split_x(1)
        split_turned(0, 0)
        act.wait_ge(const_done.sem, const_done.count(0, CONSTS))
        for m in range(4):
            keep_qk(0, m)
        keep_v(0, 0)
        keep_v(0, 1)
        body(0, ffn=False)
        body(1)
        with act.Fori(2, CHUNKS - 2) as c:
            body(c)
        body(CHUNKS - 2, prefetch=False)
        body(CHUNKS - 1, prefetch=False, front=False)
        body(CHUNKS, prefetch=False, front=False, attend=False)

    @block.vector
    def _(dve):
        SWAP = [p ^ 16 for p in range(32)]

        def moments_of(i, n, h):
            for t in range(TILES):
                dve.bn_stats(stats[i][:, t, :], h[:, t, :]).then_inc(stats_done[i].sem, 1)
            for t in range(TILES):
                value = known(dve, stats_done[i].count(n, t + 1))
                dve.wait_ge(const_done.sem, CONSTS)
                dve.wait_ge(stats_done[i].sem, value)
                dve.bn_aggr(moments[i][:, t, :], stats[i][:, t, :]).then_inc(moments_done[i].sem, 1)
            dve.wait_ge(moments_done[i].sem, moments_done[i].all(n))
            if there(n - 1):
                dve.wait_ge(rstd_done[i].sem, rstd_done[i].all(n - 1))
            dve.tensor_scalar(shifted[i][:, :], moments[i][:, :, 1], EPS, None, ALU.add).then_inc(shifted_done[i].sem, 1)

        def normalise(i, n, h):
            dve.wait_ge(rstd_done[i].sem, rstd_done[i].all(n))
            if there(n - 1):
                dve.wait_ge(turn_done[i].sem, turn_done[i].all(n - 1))
            for t in range(TILES):
                ins = dve.tensor_scalar(xn[i][:, t, :], h[:, t, :], moments[i][:, t, 0:1], rstd[i][:, t:t + 1],
                                        ALU.subtract, ALU.mult)
            ins.then_inc(xn_done[i].sem, 1)

        def split_turned(i, n):
            for k in range(KD):
                dve.wait_ge(xn_hi_done[i].sem, xn_hi_done[i].count(n, k + 1))
                dve.tensor_tensor(xn_lo[i][:, k, :], dense[k][:, 0:N], seen(xn_hi[i][:, k, :]), ALU.subtract).then_inc(xn_lo_done[i].sem, 1)

        def residual(b):
            if there(b - 1):
                dve.wait_ge(out_ready.sem, out_ready.all(b - 1))
            for u in range(2):
                dve.wait_ge(proj_done.sem, proj_done.count(b, u + 1))
                at = slice(2 * u, 2 * u + 2)
                dve.tensor_tensor(h1[:, at, :].rearrange("q t d -> q (t d)"), dense[u][0:Q, 0:2 * D],
                                  h_old[:, at, :].rearrange("q t d -> q (t d)"), ALU.add).then_inc(h1_ready.sem, 1)
            dve.wait_ge(h1_ready.sem, h1_ready.all(b))

        def move_h(c):
            dve.wait_ge(h_ready.sem, h_ready.all(c))
            dve.tensor_copy(h_old[:, :, :], h_new[:, :, :]).then_inc(h_moved.sem, 1)

        def row_max(c, f):
            image, r = divmod(f, 12)
            dve.wait_ge(fill_done.sem, fill_done.count(c, f + 1))
            if f == 0:
                if there(c - 1):
                    dve.wait_ge(max_turned.sem, max_turned.all(c - 1))
            if r < 4:
                qt, heads = 0, slice(4 * r, 4 * r + 4)
            else:
                qt, heads = 1, slice(2 * (r - 4), 2 * (r - 4) + 2)
            count, keys = heads.stop - heads.start, Q * (qt + 1)
            dve.tensor_reduce(negmax[:, heads, 2 * image + qt], score[f % 2][0:Q, 0:count * keys].rearrange("q (h k) -> q h k", h=count),
                              AX.X, ALU.max, negate=True).then_inc(max_done.sem, 1)

        def split_guard(c):
            dve.wait_ge(max_turned.sem, max_turned.all(c))
            if there(c - 1):
                dve.wait_ge(guard_loaded.sem, guard_loaded.all(c - 1))
            src = value_bank[0:HEADS * TILES, 0:Q]
            dve.tensor_copy(guard[:, 0, :], src).then_inc(guard_split.sem, 1)
            dve.wait_ge(guard_split.sem, guard_split.count(c, 1))
            dve.tensor_tensor(guard_rest[:, :], src, guard[:, 0, :], ALU.subtract).then_inc(guard_rest_done.sem, 1)
            dve.wait_ge(guard_rest_done.sem, guard_rest_done.count(c, 1))
            dve.tensor_copy(guard[:, 1, :], guard_rest[:, :]).then_inc(guard_split.sem, 1)
            dve.wait_ge(guard_split.sem, guard_split.count(c, 2))
            dve.tensor_tensor(guard[:, 2, :], guard_rest[:, :], guard[:, 1, :], ALU.subtract).then_inc(guard_split.sem, 1)
            dve.wait_ge(guard_split.sem, guard_split.count(c, 3))
            dve.memset(guard_rest[0:1, 0:1], 0.0).then_inc(guard_rest_done.sem, 1)

        def swap(n, side):
            ready = known(dve, qk_ready.count(n, 2 * side + 2))
            summed = known(dve, rope_done.all(n - 1)) if side == 0 and there(n - 1) else None
            dve.wait_ge(const_done.sem, CONSTS)
            dve.wait_ge(qk_ready.sem, ready)
            if summed is not None:
                dve.wait_ge(rope_done.sem, summed)
            dve.stream_shuffle(turned[:, side, :], qk[:, 2 * side + 1, :], SWAP).then_inc(swapped_done.sem, 1)

        def rotate(n, side):
            dve.wait_ge(cos_done.sem, cos_done.count(n, side + 1))
            dve.wait_ge(sin_done.sem, sin_done.count(n, side + 1))
            dve.tensor_tensor(qk[:, 2 * side + 1, :], qk[:, 2 * side + 1, :], turned[:, side, :], ALU.add).then_inc(rope_done.sem, 1)

        def split_qk(n, side):
            at = slice(2 * side, 2 * side + 2)
            dve.wait_ge(rope_done.sem, rope_done.count(n, side + 1))
            if side == 0:
                if there(n - 1):
                    dve.wait_ge(stack_loaded.sem, stack_loaded.all(n - 1))
            dve.tensor_copy(part[0][:, at, :], qk[:, at, :]).then_inc(part0_done.sem, 1)
            dve.wait_ge(part0_done.sem, part0_done.count(n, side + 1))
            dve.tensor_tensor(qk[:, at, :], qk[:, at, :], part[0][:, at, :], ALU.subtract).then_inc(rest_done.sem, 1)
            dve.wait_ge(rest_done.sem, rest_done.count(n, side + 1))
            dve.tensor_copy(part[1][:, at, :], qk[:, at, :]).then_inc(part1_done.sem, 1)
            dve.wait_ge(part1_done.sem, part1_done.count(n, side + 1))
            dve.tensor_tensor(part[2][:, at, :], qk[:, at, :], part[1][:, at, :], ALU.subtract).then_inc(part2_done.sem, 1)

        def keep_sums(c, quad):
            dve.wait_ge(pv_done.sem, pv_done.count(c, 2 * quad + 2))
            if quad == 0:
                if there(c - 1):
                    dve.wait_ge(y_loaded.sem, y_loaded.all(c - 1))
            dve.tensor_copy(o_sums[:, quad, :], value_banks[quad % 2][:, 0:N]).then_inc(o_ready.sem, 1)

        def divide(c):
            dve.wait_ge(y_loaded.sem, y_loaded.all(c))
            dve.reciprocal(den[:, :, :], den[:, :, :]).then_inc(recip_done.sem, 1)
            dve.wait_ge(recip_done.sem, recip_done.all(c))
            dve.tensor_tensor(y[:, :, :], y[:, :, :], den[:, :, :], ALU.mult).then_inc(y_done.sem, 1)

        def split_g(b):
            for m in range(KH):
                dve.wait_ge(gelu_done.sem, gelu_done.count(b, m + 1))
                if m == 0:
                    if there(b - 1):
                        dve.wait_ge(down_done.sem, down_done.all(b - 1))
                dve.tensor_copy(g_hi[:, m, :], g[:, m % 2, :]).then_inc(g_hi_done.sem, 1)
                if m % 2:
                    dve.wait_ge(g_hi_done.sem, g_hi_done.count(b, m + 1))
                    dve.tensor_tensor(g_lo[:, m, :], g[:, m % 2, :], seen(g_hi[:, m, :]), ALU.subtract).then_inc(g_lo_odd.sem, 1)

        def scale(b):
            if there(b - 1):
                dve.wait_ge(out_stored.sem, out_stored.all(b - 1))
            for u in range(2):
                dve.wait_ge(down_done.sem, down_done.count(b, u + 1))
                dve.tensor_tensor(out[:, 2 * u:2 * u + 2, :], dense[u][0:Q, 0:2 * D].rearrange("q (t d) -> q t d", t=2),
                                  w["alpha2"][:, :].unsqueeze(1).to_broadcast([Q, 2, D]), ALU.mult).then_inc(scaled_done.sem, 1)

        def body(c, attend=True, front=True, ffn=True, prefetch=True):
            n, b = c + 1, c - 1
            if ffn:
                residual(b)
                moments_of(1, b, h1)
            if attend:
                move_h(c)
                for f in range(FILLS):
                    row_max(c, f)
                    if f == 3 and ffn:
                        normalise(1, b, h1)
                    if f == 19 and front:
                        dve.wait_ge(h_ready.sem, h_ready.all(n))
                        moments_of(0, n, h_new)
            elif ffn:
                normalise(1, b, h1)
            if front:
                normalise(0, n, h_new)
            if attend:
                split_guard(c)
            if ffn:
                split_turned(1, b)
            if front:
                split_turned(0, n)
                swap(n, 0)
            if attend:
                keep_sums(c, 0)
            if front:
                rotate(n, 0)
                split_qk(n, 0)
            if attend:
                keep_sums(c, 1)
            if front:
                swap(n, 1)
            if attend:
                keep_sums(c, 2)
            if front:
                rotate(n, 1)
                split_qk(n, 1)
            if attend:
                keep_sums(c, 3)
            if ffn:
                split_g(b)
            if attend:
                divide(c)
            if ffn:
                scale(b)

        dve.memset(k_stack[ROWS:ROWS + GUARD, :, :], 1.0).then_inc(const_done.sem, 1)
        dve.memset(values[:, :, 1, :, :], 0.0).then_inc(const_done.sem, 1)
        dve.memset(e_near[:, :, :, :], 0.0).then_inc(const_done.sem, 1)
        dve.memset(values[:, :, 0, :, DH:2 * DH], 1.0).then_inc(const_done.sem, 1)
        dve.wait_ge(const_done.sem, const_done.count(0, 2))
        dve.memset(values[0:KEYS[1], :, 1, :, DH:2 * DH], 1.0).then_inc(const_done.sem, 1)
        dve.wait_ge(h_ready.sem, h_ready.all(0))
        moments_of(0, 0, h_new)
        normalise(0, 0, h_new)
        split_turned(0, 0)
        for side in range(2):
            swap(0, side)
            rotate(0, side)
            split_qk(0, side)
        body(0, ffn=False)
        body(1)
        with dve.Fori(2, CHUNKS - 2) as c:
            body(c)
        body(CHUNKS - 2, prefetch=False)
        body(CHUNKS - 1, prefetch=False, front=False)
        body(CHUNKS, prefetch=False, front=False, attend=False)

    @block.gpsimd
    def _(pool):
        def power(i, n):
            pool.wait_ge(shifted_done[i].sem, shifted_done[i].all(n))
            if there(n - 1):
                pool.wait_ge(xn_done[i].sem, xn_done[i].all(n - 1))
            pool.tensor_tensor(rstd[i][:, :], shifted[i][:, :], w["minus_half"][:, :], ALU.pow).then_inc(rstd_done[i].sem, 1)

        def bias(b):
            pool.wait_ge(xn_done[1].sem, xn_done[1].all(b))
            pool.tensor_tensor(h1[:, :, :], h1[:, :, :], w["b2"][:, :].unsqueeze(1).to_broadcast([Q, TILES, D]),
                               ALU.add).then_inc(h1_biased.sem, 1)

        def split_x(m, half):
            pool.wait_ge(x_hi_done.sem, x_hi_done.count(m, half + 1))
            if there(m - 1):
                pool.wait_ge(tok_done.sem, tok_done.all(m - 1))
            at = slice(half * KF // 2, (half + 1) * KF // 2)
            pool.tensor_tensor(x_lo[:, at, :], x_raw[:, at, :], seen(x_hi[:, at, :]), ALU.subtract).then_inc(x_lo_done.sem, 1)

        def times_tables(n, side):
            pool.wait_ge(swapped_done.sem, swapped_done.count(n, side + 1))
            pool.tensor_tensor(qk[:, 2 * side + 1, :], qk[:, 2 * side + 1, :], w["cos"][:, :], ALU.mult).then_inc(cos_done.sem, 1)
            pool.tensor_tensor(turned[:, side, :], turned[:, side, :], w["sin"][:, :], ALU.mult).then_inc(sin_done.sem, 1)

        def mask(c, i):
            value = known(pool, exp_far.count(c, 2 * i + 2))
            pool.wait_ge(const_done.sem, CONSTS)
            pool.wait_ge(exp_far.sem, value)
            tile = e_far[:, i % 2, :, 0:P]
            pool.affine_select(out=tile, in_=tile, compare_op=ALU.is_ge, fill=0.0, base=0,
                               pattern=[[0, 4], [1, P]], channel_multiplier=-1).then_inc(masked_done.sem, 1)
            value = known(pool, exp_near.count(c, i + 1))
            pool.wait_ge(const_done.sem, CONSTS)
            pool.wait_ge(exp_near.sem, value)
            tile = e_near[0:KEYS[1], i % 2, :, :]
            pool.affine_select(out=tile, in_=tile, compare_op=ALU.is_ge, fill=0.0, base=0,
                               pattern=[[0, 4], [1, KEYS[1]]], channel_multiplier=-1).then_inc(masked_done.sem, 1)

        def split_g(b):
            for m in range(0, KH, 2):
                pool.wait_ge(g_hi_done.sem, g_hi_done.count(b, m + 1))
                pool.tensor_tensor(g_lo[:, m, :], g[:, 0, :], seen(g_hi[:, m, :]), ALU.subtract).then_inc(g_lo_even.sem, 1)

        def split_y(c):
            pool.wait_ge(y_hi_done.sem, y_hi_done.all(c))
            for k in range(KD):
                pool.tensor_tensor(y_lo[:, k, :], y[:, k, :], seen(y_hi[:, k, :]), ALU.subtract).then_inc(y_lo_done.sem, 1)

        def finish(b):
            pool.wait_ge(h1_biased.sem, h1_biased.all(b))
            for u in range(2):
                pool.wait_ge(scaled_done.sem, scaled_done.count(b, u + 1))
                at = slice(2 * u, 2 * u + 2)
                pool.tensor_tensor(out[:, at, :], out[:, at, :], h1[:, at, :], ALU.add).then_inc(out_ready.sem, 1)

        def body(c, attend=True, front=True, ffn=True, prefetch=True):
            n, b = c + 1, c - 1
            if ffn:
                power(1, b)
                bias(b)
            if front:
                power(0, n)
            if prefetch:
                split_x(c + 2, 0)
            if attend:
                for i in range(G):
                    mask(c, i)
                    if front and i == 0:
                        times_tables(n, 0)
                    if front and i == 4:
                        times_tables(n, 1)
            if prefetch:
                split_x(c + 2, 1)
            if ffn:
                split_g(b)
            if attend:
                split_y(c)
            if ffn:
                finish(b)

        split_x(0, 0)
        split_x(0, 1)
        power(0, 0)
        split_x(1, 0)
        split_x(1, 1)
        times_tables(0, 0)
        times_tables(0, 1)
        body(0, ffn=False)
        body(1)
        with pool.Fori(2, CHUNKS - 2) as c:
            body(c)
        body(CHUNKS - 2, prefetch=False)
        body(CHUNKS - 1, prefetch=False, front=False)
        body(CHUNKS, prefetch=False, front=False, attend=False)


def kernel(**inputs):
    import concourse.bacc as _bacc
    from concourse.bass_utils import run_bass_kernel_spmd as _run

    a = {k: np.asarray(v) for k, v in inputs.items()}
    side = SIDE // PATCH
    x = a["x"].reshape(IMAGES, CHANNELS, side, PATCH, side, PATCH).transpose(0, 1, 3, 5, 2, 4).reshape(IMAGES, T, F)
    x = x.reshape(CHUNKS, N, KF, P).transpose(0, 3, 2, 1)

    def tiles(m):
        return m.reshape(-1, P, m.shape[1]).transpose(1, 0, 2)

    down = np.stack([a[f"L0_attn_W{s}_down"].reshape(D, HEADS, LATENT).transpose(2, 1, 0) for s in "qkv"])
    up = np.stack([np.concatenate([a["L0_attn_Wq_up_c"], a["L0_attn_Wq_up_e"]], 1),
                   np.concatenate([a["L0_attn_Wk_up_c"], a["L0_attn_Wk_up_e"]], 1), a["L0_attn_Wv_up"]], 1)
    w1, w2 = a["L0_ffn_w1"], a["L0_ffn_w2"]
    inv = (1.0 / np.float32(THETA) ** (np.arange(0, DR, 2, dtype=np.float32) / np.float32(DR))).astype(np.float32)
    angle = np.arange(T, dtype=np.float32)[:, None] * np.concatenate([inv, inv])[None, :]
    cos = np.repeat(np.tile(np.cos(angle).T, (1, PER)), HEADS, axis=0)
    sin = np.repeat(np.tile(np.sin(angle).T * np.where(np.arange(DR) % 2, 1.0, -1.0)[:, None], (1, PER)), HEADS, axis=0)
    mask = np.tile(np.where(np.tril(np.ones((Q, Q), bool)), 0.0, MASKED), (1, 4))
    arrays = {
        "x_in": x, "tok_in": tiles(a["L0_tok_W"]), "down_in": down, "up_in": up, "wc_in": tiles(a["L0_attn_Wc"]),
        "w1t_in": tiles(w1.T).reshape(P, KD * HID), "w1_in": tiles(w1), "b1_in": a["L0_ffn_b1"].reshape(KH, P).T,
        "w2t_in": tiles(w2.T).reshape(P, KH * D), "b2_in": np.broadcast_to(a["L0_ffn_b2"], (Q, D)),
        "cos_in": cos.astype(np.float32), "sin_in": sin.astype(np.float32), "mask_in": mask.astype(np.float32),
        "ident_in": np.eye(Q, dtype=np.float32),
    }
    arrays = {k: np.ascontiguousarray(v) for k, v in arrays.items()}
    nc = _bacc.Bacc("TRN2", target_bir_lowering=False, num_devices=1, dynamic_dma_scratch_size=1024)
    args = [nc.dram_tensor(k, v.shape, mybir.dt.from_np(v.dtype), kind="ExternalInput").ap() for k, v in arrays.items()]
    y = nc.dram_tensor("y_out", (CHUNKS, TILES, Q, D), FP32, kind="ExternalOutput").ap()
    vit_layer(nc, *args, y)
    r = _run(nc, [arrays], core_ids=[0])
    return r.results[0]["y_out"].reshape(IMAGES, T, D)
```

```python
import math

import numpy as np

import concourse.bass as bass
from concourse import mybir
from contextlib import ExitStack

FP32 = mybir.dt.float32
FP32R = mybir.dt.float32r
BF16 = mybir.dt.bfloat16
ALU = mybir.AluOpType
ACT = mybir.ActivationFunctionType
AX = mybir.AxisListType

IMAGES, CHANNELS, SIDE, PATCH = 64, 3, 224, 16
T = (SIDE // PATCH) ** 2
F = CHANNELS * PATCH * PATCH
D = 256
HEADS, LATENT, DH = 16, 64, 16
DR = DH // 2
HID = 1024
THETA, EPS = 10000.0, 1e-5

P = 128
PER = 2
CHUNKS = IMAGES // PER
N = PER * T
Q = T // 2
TILES = N // Q
KF, KD, KH = F // P, D // P, HID // P
KEYS = (P, T - P)
COMBOS = ((0, 0), (1, 0), (2, 0), (0, 1), (1, 1), (0, 2))
ROWS = len(COMBOS) * DH
GUARD = 3
QUADS = HEADS // 4
MASKED = -1e30
E_SLOTS = 3
G_SLOTS = 4


def vit_layer(nc, x_in, tok_in, down_in, up_in, wc_in, w1t_in, w1_in, b1_in, w2t_in, b2_in,
              cos_in, sin_in, mask_in, ident_in, y_out):
    with ExitStack() as ctx:
        def sb(name, shape, dt=FP32):
            return ctx.enter_context(nc.sbuf_tensor(name, shape, dt))

        tok_hi, tok_lo = sb("tok_hi", [P, KF, D], FP32R), sb("tok_lo", [P, KF, D], FP32R)
        wqk_hi, wqk_lo = sb("wqk_hi", [P, KD, 2 * D], FP32R), sb("wqk_lo", [P, KD, 2 * D], FP32R)
        wv_hi, wv_lo = sb("wv_hi", [P, KD, D], FP32R), sb("wv_lo", [P, KD, D], FP32R)
        wc_hi, wc_lo = sb("wc_hi", [P, KD, D], FP32R), sb("wc_lo", [P, KD, D], FP32R)
        sign1 = sb("sign1", [P, KD, HID], FP32R)
        sign2 = sb("sign2", [P, KH, D], FP32R)
        alpha1, b1 = sb("alpha1", [P, KH]), sb("b1", [P, KH])
        alpha2, b2 = sb("alpha2", [Q, D]), sb("b2", [Q, D])
        cos, sin = sb("cos", [P, N]), sb("sin", [P, N])
        ident = sb("ident", [Q, Q])
        ident_bf, mask_bf = sb("ident_bf", [Q, Q], BF16), sb("mask_bf", [Q, 4 * Q], BF16)
        minus_half = sb("minus_half", [Q, TILES])

        prepare_weights(nc, locals())
        run_chunks(nc, ctx, sb, locals())


def prepare_weights(nc, w):
    with ExitStack() as ctx:
        def sb(name, shape, dt=FP32):
            return ctx.enter_context(nc.sbuf_tensor(name, shape, dt))

        def sem(name):
            return ctx.enter_context(nc.semaphore(name))

        tok = sb("tok_raw", [P, KF, D])
        down = [sb(f"down_{s}", [LATENT, HEADS, D]) for s in "qkv"]
        up = sb("up", [LATENT, 3, DH])
        wc = sb("wc_raw", [P, KD, D])
        w1t, w1, w2t = sb("w1t", [P, KD * HID]), sb("w1", [P, KH, D]), sb("w2t", [P, KH * D])
        negative1, negative2 = sb("negative1", [P, KD * HID]), sb("negative2", [P, KH * D])
        abs2 = sb("abs2", [P, KH, D])
        ones = sb("ones", [P, Q])
        mask = sb("mask", [Q, 4 * Q])
        folded = [ctx.enter_context(nc.psum_tensor(f"folded{i}", [P, 512], FP32)) for i in range(6)]
        mean2 = ctx.enter_context(nc.psum_tensor("mean2", [Q, D], FP32))

        loads = [(tok, w["tok_in"]), (w1t, w["w1t_in"]), (w1, w["w1_in"]), (w2t, w["w2t_in"]),
                 (wc, w["wc_in"]), (w["b1"], w["b1_in"]), (w["b2"], w["b2_in"]), (w["cos"], w["cos_in"]),
                 (w["sin"], w["sin_in"]), (mask, w["mask_in"]), (w["ident"], w["ident_in"])]
        weights_loaded, latent_loaded = sem("weights_loaded"), sem("latent_loaded")
        fold_done, ones_set, abs_done, mean_done = sem("fold_done"), sem("ones_set"), sem("abs_done"), sem("mean_done")
        hi_done, negative_done, sum_done, prep_done = sem("hi_done"), sem("negative_done"), sem("sum_done"), sem("prep_done")
        block = ctx.enter_context(nc.Block())

        @block.sync
        def _(sp):
            for s in range(3):
                sp.dma_start(down[s][:, :, :], w["down_in"][s]).then_inc(latent_loaded, 16)
            sp.dma_start(up[:, :, :], w["up_in"]).then_inc(latent_loaded, 16)
            for to, of in loads:
                sp.dma_start(to[tuple(slice(None) for _ in to.shape)], of).then_inc(weights_loaded, 16)

        @block.tensor
        def _(pe):
            pe.wait_ge(latent_loaded, 4 * 16)
            for s in range(3):
                for k in range(KD):
                    for h in range(HEADS):
                        bank = folded[2 * s + k]
                        out = bank[:, h:D:HEADS] if s < 2 else bank[:, h * DH:(h + 1) * DH]
                        mm = pe.matmul(out, down[s][:, h, k * P:(k + 1) * P], up[:, s, :], start=True, stop=True)
                    mm.then_inc(fold_done, 1)
            pe.wait_ge(ones_set, 1)
            pe.wait_ge(abs_done, 1)
            for k in range(KH):
                mm = pe.matmul(mean2[:, :], ones[:, :], abs2[:, k, :], start=(k == 0), stop=(k == KH - 1))
            mm.then_inc(mean_done, 1)

        @block.vector
        def _(dve):
            dve.memset(ones[:, :], 1.0).then_inc(ones_set, 1)
            dve.memset(w["minus_half"][:, :], -0.5)
            dve.wait_ge(weights_loaded, len(loads) * 16)
            dve.scalar_tensor_tensor(out=abs2[:, :, :].rearrange("p k d -> p (k d)"), in0=w2t[:, :], scalar=-1.0,
                                     in1=w2t[:, :], op0=ALU.mult, op1=ALU.max).then_inc(abs_done, 1)
            for n, (negative, raw) in enumerate(((negative1, w1t), (negative2, w2t))):
                dve.tensor_scalar(negative[:, :], raw[:, :], 0.0, None, ALU.is_lt).then_inc(negative_done, 1)
            for n, (negative, raw, out) in enumerate(((negative1, w1t, w["sign1"]), (negative2, w2t, w["sign2"]))):
                dve.wait_ge(negative_done, n + 1)
                dve.scalar_tensor_tensor(out=out[:, :, :].rearrange("p k d -> p (k d)"), in0=raw[:, :], scalar=0.0,
                                         in1=negative[:, :], op0=ALU.is_gt, op1=ALU.subtract).then_inc(prep_done, 1)
            dve.tensor_reduce(w["alpha1"][:, :], w1[:, :, :], AX.X, ALU.add,
                              apply_absolute_value=True).then_inc(sum_done, 1)
            dve.tensor_copy(w["ident_bf"][:, :], w["ident"][:, :]).then_inc(prep_done, 1)
            dve.tensor_copy(w["mask_bf"][:, :], mask[:, :]).then_inc(prep_done, 1)
            dve.wait_ge(sum_done, 1)
            dve.tensor_scalar(w["alpha1"][:, :], w["alpha1"][:, :], 1.0 / D, None, ALU.mult).then_inc(prep_done, 1)
            dve.tensor_copy(w["tok_hi"][:, :, :], tok[:, :, :]).then_inc(hi_done, 1)
            dve.tensor_copy(w["wc_hi"][:, :, :], wc[:, :, :]).then_inc(hi_done, 1)
            dve.wait_ge(hi_done, 1)
            dve.tensor_tensor(w["tok_lo"][:, :, :], tok[:, :, :], w["tok_hi"][:, :, :].bitcast(FP32),
                              ALU.subtract).then_inc(prep_done, 1)
            dve.wait_ge(hi_done, 2)
            dve.tensor_tensor(w["wc_lo"][:, :, :], wc[:, :, :], w["wc_hi"][:, :, :].bitcast(FP32),
                              ALU.subtract).then_inc(prep_done, 1)
            parts = []
            for s in range(3):
                for k in range(KD):
                    at = slice(s * D, (s + 1) * D) if s < 2 else slice(0, D)
                    parts.append((folded[2 * s + k][:, 0:D], DH ** -0.5 if s == 0 else 1.0,
                                  (w["wqk_hi"] if s < 2 else w["wv_hi"])[:, k, at],
                                  (w["wqk_lo"] if s < 2 else w["wv_lo"])[:, k, at]))
            for n, (psum, scale, hi, lo) in enumerate(parts):
                dve.wait_ge(fold_done, n + 1)
                dve.tensor_scalar(hi, psum, scale, None, ALU.mult).then_inc(hi_done, 1)
                dve.wait_ge(hi_done, n + 3)
                dve.scalar_tensor_tensor(out=lo, in0=psum, scalar=scale, in1=hi.bitcast(FP32),
                                         op0=ALU.mult, op1=ALU.subtract).then_inc(prep_done, 1)
            dve.wait_ge(mean_done, 1)
            dve.tensor_scalar(w["alpha2"][:, :], mean2[:, :], 1.0 / HID, None, ALU.mult).then_inc(prep_done, 1)
            dve.wait_ge(prep_done, 2 + 3 + 2 + len(parts) + 1)


class Event:

    def __init__(self, ctx, nc, name, per):
        self.sem, self.per = ctx.enter_context(nc.semaphore(name)), per

    def count(self, chunk, k):
        return chunk * self.per + k

    def all(self, chunk):
        return (chunk + 1) * self.per


def there(chunk):
    return not isinstance(chunk, int) or chunk >= 0


def known(eng, value):
    return value if isinstance(value, int) else eng.to_reg(value)


def run_chunks(nc, ctx, sb, w):
    DMA = 16

    def event(name, per):
        return Event(ctx, nc, name, per)

    x_raw = sb("x_raw", [P, KF, N])
    x_hi, x_lo = sb("x_hi", [P, KF, N], FP32R), sb("x_lo", [P, KF, N], FP32R)
    h_new, h_next, h_now, h1 = (sb("h_new", [Q, TILES, D]), sb("h_next", [Q, TILES, D]),
                                sb("h_now", [Q, TILES, D]), sb("h1", [Q, TILES, D]))
    stats = [sb(f"stats{i}", [Q, TILES, 6]) for i in range(2)]
    moments = [sb(f"moments{i}", [Q, TILES, 2]) for i in range(2)]
    shifted = [sb(f"shifted{i}", [Q, TILES]) for i in range(2)]
    rstd = [sb(f"rstd{i}", [Q, TILES]) for i in range(2)]
    xn = [sb(f"xn{i}", [Q, TILES, D]) for i in range(2)]
    xn_hi = [sb(f"xn_hi{i}", [P, KD, N], FP32R) for i in range(2)]
    xn_lo = [sb(f"xn_lo{i}", [P, KD, N], FP32R) for i in range(2)]
    qk = sb("qk", [P, 4, N])
    turned = sb("turned", [P, 2, N])
    part = [sb(f"part{i}", [P, 4, N], BF16) for i in range(3)]
    q_stack = sb("q_stack", [ROWS + GUARD, HEADS, N], BF16)
    k_stack = sb("k_stack", [ROWS + GUARD, HEADS, N], BF16)
    negmax = sb("negmax", [Q, HEADS, TILES])
    guard = sb("guard", [HEADS * TILES, GUARD, Q], BF16)
    guard_rest = sb("guard_rest", [HEADS * TILES, Q])
    e_far = sb("e_far", [P, E_SLOTS, 4, T])
    e_near = sb("e_near", [P, E_SLOTS, 4, KEYS[1]])
    values = sb("values", [P, PER, 2, HEADS, 2 * DH])
    o_sums = sb("o_sums", [P, QUADS, N])
    y_hi, y_lo = sb("y_hi", [P, KD, N], FP32R), sb("y_lo", [P, KD, N], FP32R)
    g = sb("g", [P, G_SLOTS, N])
    den, y = g[:, 0:KD, :], g[:, KD:2 * KD, :]
    g_hi, g_lo = sb("g_hi", [P, KH, N], FP32R), sb("g_lo", [P, KH, N], FP32R)

    def bank(name):
        return ctx.enter_context(nc.psum_tensor(name, [P, 512], FP32))

    dense = [bank("dense0"), bank("dense1")]
    score = [bank("score0"), bank("score1")]
    far = [bank("far0"), bank("far1")]
    near = bank("near")
    value_bank = bank("value_bank")
    value_banks = [value_bank, score[0]]
    far_banks = [far[0], far[1], score[1]]
    token_banks = [dense[0], near]
    up_banks = [far[0], far[1], dense[0], dense[1]]

    x_loaded = event("x_loaded", DMA)
    x_hi_done, x_lo_done = event("x_hi_done", 2), event("x_lo_done", 2)
    tok_done, h_ready = event("tok_done", 2), event("h_ready", 2)
    in_next, in_now, in_h1 = event("in_next", 1), event("in_now", 1), event("in_h1", 1)
    stats_done = [event(f"stats_done{i}", TILES) for i in range(2)]
    moments_done = [event(f"moments_done{i}", TILES) for i in range(2)]
    shifted_done = [event(f"shifted_done{i}", 1) for i in range(2)]
    rstd_done = [event(f"rstd_done{i}", 1) for i in range(2)]
    xn_done = [event(f"xn_done{i}", 1) for i in range(2)]
    turn_done = [event(f"turn_done{i}", KD) for i in range(2)]
    xn_hi_done = [event(f"xn_hi_done{i}", KD) for i in range(2)]
    xn_lo_done = [event(f"xn_lo_done{i}", KD) for i in range(2)]
    qk_mm_done, qk_ready = event("qk_mm_done", 4), event("qk_ready", 4)
    swapped_done, cos_done, sin_done, rope_done = (event("swapped_done", 2), event("cos_done", 2),
                                                   event("sin_done", 2), event("rope_done", 2))
    part0_done, rest_done, part1_done, part2_done = (event("part0_done", 2), event("rest_done", 2),
                                                     event("part1_done", 2), event("part2_done", 2))
    stack_loaded = event("stack_loaded", 4 * len(COMBOS) * DMA)
    v_mm_done, v_ready = event("v_mm_done", PER), event("v_ready", PER * 2)
    FILLS = PER * (4 + 8)
    fill_done, max_done = event("fill_done", FILLS), event("max_done", FILLS)
    max_turned, guard_split, guard_rest_done, guard_loaded = (event("max_turned", 1), event("guard_split", 3),
                                                              event("guard_rest_done", 2), event("guard_loaded", GUARD * DMA))
    G = QUADS * PER
    far_done, near_done = event("far_done", 2 * G), event("near_done", G)
    exp_far, exp_near = event("exp_far", 2 * G), event("exp_near", G)
    masked_done, pv_done, o_ready = event("masked_done", 2 * G), event("pv_done", G), event("o_ready", QUADS)
    y_loaded = event("y_loaded", 16 * DMA)
    recip_done, y_done, y_hi_done, y_lo_done = (event("recip_done", 1), event("y_done", 1),
                                                event("y_hi_done", 1), event("y_lo_done", KD))
    proj_done, h1_ready, h1_biased = event("proj_done", 2), event("h1_ready", 2), event("h1_biased", 1)
    up_done, gelu_done, g_hi_done, g_lo_even, g_lo_odd = (event("up_done", KH), event("gelu_done", KH),
                                                          event("g_hi_done", KH), event("g_lo_even", KH // 2),
                                                          event("g_lo_odd", KH // 2))
    down_done, scaled_done, out_ready, out_stored = (event("down_done", 2), event("scaled_done", 2),
                                                     event("out_ready", 2), event("out_stored", DMA))
    const_done = event("const_done", 1)
    CONSTS = 5

    def seen(x):
        return x.bitcast(FP32)


    block = ctx.enter_context(nc.Block())

    @block.sync
    def _(sp):
        def load_x(m, prev):
            src = w["x_in"][m] if isinstance(m, int) else w["x_in"][bass.ds(sp.snap(m), 1)].rearrange("a p k n -> (a p) k n")
            value0 = known(sp, x_hi_done.all(prev)) if there(prev) else 0
            value1 = known(sp, x_lo_done.all(prev)) if there(prev) else 0
            sp.wait_ge(const_done.sem, CONSTS)
            if there(prev):
                sp.wait_ge(x_hi_done.sem, value0)
            if there(prev):
                sp.wait_ge(x_lo_done.sem, value1)
            sp.dma_start(x_raw[:, :, :], src).then_inc(x_loaded.sem, 16)

        def load_guard(c):
            for r in range(GUARD):
                value = known(sp, guard_split.count(c, r + 1))
                sp.wait_ge(const_done.sem, CONSTS)
                sp.wait_ge(guard_split.sem, value)
                sp.dma_start(q_stack[ROWS + r:ROWS + r + 1, :, :], guard[:, r, :]).then_inc(guard_loaded.sem, 16)

        def load_y(c):
            hi_split = known(sp, g_hi_done.all(c - 1)) if there(c - 1) else 0
            even_split = known(sp, g_lo_even.all(c - 1)) if there(c - 1) else 0
            odd_split = known(sp, g_lo_odd.all(c - 1)) if there(c - 1) else 0
            summed = known(sp, o_ready.all(c))
            sp.wait_ge(const_done.sem, CONSTS)
            if there(c - 1):
                sp.wait_ge(g_hi_done.sem, hi_split)
                sp.wait_ge(g_lo_even.sem, even_split)
                sp.wait_ge(g_lo_odd.sem, odd_split)
            sp.wait_ge(o_ready.sem, summed)
            for odd in range(2):
                for j in range(4):
                    rows = slice(odd * 64 + j * DH, odd * 64 + (j + 1) * DH)
                    sp.dma_start(den[rows, :, :], o_sums[32 * j + DH:32 * j + 2 * DH, odd:QUADS:2, :]).then_inc(y_loaded.sem, 16)
                    sp.dma_start(y[rows, :, :], o_sums[32 * j:32 * j + DH, odd:QUADS:2, :]).then_inc(y_loaded.sem, 16)

        def load_stack(n, c):
            value0 = known(sp, far_done.all(c)) if there(c) else 0
            value1 = known(sp, near_done.all(c)) if there(c) else 0
            sp.wait_ge(const_done.sem, CONSTS)
            if there(c):
                sp.wait_ge(far_done.sem, value0)
            if there(c):
                sp.wait_ge(near_done.sem, value1)
            for i, made in enumerate((part0_done, part1_done, part2_done)):
                value = known(sp, made.all(n))
                sp.wait_ge(const_done.sem, CONSTS)
                sp.wait_ge(made.sem, value)
                for r, (of_q, of_k) in enumerate(COMBOS):
                    for side, stack, of in ((0, q_stack, of_q), (1, k_stack, of_k)):
                        if of != i:
                            continue
                        for rotary in range(2):
                            row = r * DH + rotary * DR
                            sp.dma_start(stack[row:row + DR, :, :], part[i][:, 2 * side + rotary, :]).then_inc(stack_loaded.sem, 16)

        def store(b):
            dst = (w["y_out"][b] if isinstance(b, int) else w["y_out"][bass.ds(sp.snap(b), 1)].rearrange("a t p d -> (a t) p d"))
            value = known(sp, out_ready.all(b))
            sp.wait_ge(const_done.sem, CONSTS)
            sp.wait_ge(out_ready.sem, value)
            sp.dma_start(dst.rearrange("t p d -> p t d"), h1[:, :, :]).then_inc(out_stored.sem, 16)

        def body(c, attend=True, front=True, tok=True, prefetch=True, ffn=True):
            if prefetch:
                load_x(c + 3, c + 2)
            if attend:
                load_guard(c)
            if front:
                load_stack(c + 1, c)
            if attend:
                load_y(c)
            if ffn:
                store(c - 1)

        load_x(0, -1)
        load_x(1, 0)
        load_x(2, 1)
        load_stack(0, -1)
        body(0, ffn=False)
        body(1)
        with sp.Fori(2, CHUNKS - 3) as c:
            body(c)
        body(CHUNKS - 3, prefetch=False)
        body(CHUNKS - 2, prefetch=False, tok=False)
        body(CHUNKS - 1, prefetch=False, tok=False, front=False)
        body(CHUNKS, prefetch=False, tok=False, front=False, attend=False)
        sp.wait_ge(out_stored.sem, out_stored.all(CHUNKS - 1))

    @block.tensor
    def _(pe):
        def tokens(n, piece):
            t, half = divmod(piece, 2)
            if piece == 0:
                pe.wait_ge(x_hi_done.sem, x_hi_done.all(n))
                pe.wait_ge(x_lo_done.sem, x_lo_done.all(n))
                if there(n - 1):
                    pe.wait_ge(qk_ready.sem, qk_ready.count(n - 1, 3))
            if piece == 4 and there(n - 2):
                pe.wait_ge(exp_near.sem, exp_near.all(n - 2))
            if piece == 4 and there(n - 1) and not there(n - 2):
                pe.wait_ge(h_ready.sem, h_ready.all(n - 1))
            steps = [(k, a, b) for k in range(KF) for a, b in ((x_hi, w["tok_hi"]), (x_lo, w["tok_hi"]), (x_hi, w["tok_lo"]))]
            for i in range(9 * half, 9 * half + 9):
                k, a, b = steps[i]
                mm = pe.matmul(token_banks[t // 2][0:Q, (t % 2) * D:(t % 2 + 1) * D], a[:, k, t * Q:(t + 1) * Q], b[:, k, :],
                               start=(i == 0), stop=(i == len(steps) - 1))
            if piece % 4 == 3:
                mm.then_inc(tok_done.sem, 1)

        def turn_ffn(b, front):
            pe.wait_ge(xn_done[1].sem, xn_done[1].all(b))
            for k in range(KD):
                if front:
                    pe.wait_ge(v_ready.sem, v_ready.count(b + 2, 2 * (k + 1)))
                else:
                    pe.wait_ge(h1_ready.sem, h1_ready.count(b, k + 1))
                for t in range(TILES):
                    mm = pe.transpose(dense[k][:, t * Q:(t + 1) * Q], xn[1][:, t, k * P:(k + 1) * P], w["ident"][:, :])
                mm.then_inc(turn_done[1].sem, 1)

        def turn_front(n):
            pe.wait_ge(xn_done[0].sem, xn_done[0].all(n))
            if not isinstance(n, int) or n > 2:
                pe.wait_ge(scaled_done.sem, scaled_done.all(n - 3))
            elif n > 0:
                pe.wait_ge(v_ready.sem, v_ready.all(n - 1))
            else:
                pe.wait_ge(h_ready.sem, h_ready.all(0))
            for k in range(KD):
                for t in range(TILES):
                    mm = pe.transpose(dense[k][:, t * Q:(t + 1) * Q], xn[0][:, t, k * P:(k + 1) * P], w["ident"][:, :])
                mm.then_inc(turn_done[0].sem, 1)

        def project_qk(n, m):
            if m == 0:
                pe.wait_ge(xn_hi_done[0].sem, xn_hi_done[0].all(n))
                pe.wait_ge(xn_lo_done[0].sem, xn_lo_done[0].all(n))
            if m >= 2:
                pe.wait_ge(qk_ready.sem, qk_ready.count(n, m - 1))
            steps = [(k, a, b) for k in range(KD) for a, b in ((w["wqk_hi"], xn_hi[0]), (w["wqk_lo"], xn_hi[0]), (w["wqk_hi"], xn_lo[0]))]
            for i, (k, a, b) in enumerate(steps):
                mm = pe.matmul(dense[m % 2][:, 0:N], a[:, k, m * P:(m + 1) * P], b[:, k, :],
                               start=(i == 0), stop=(i == len(steps) - 1))
            mm.then_inc(qk_mm_done.sem, 1)

        def project_v(n, image, ffn):
            if ffn:
                pe.wait_ge(h1_ready.sem, h1_ready.count(n - 2, image + 1))
            elif image == 0:
                pe.wait_ge(h_ready.sem, h_ready.count(n + 1, 1))
            else:
                pe.wait_ge(qk_ready.sem, qk_ready.count(n, 4))
            steps = [(k, a, b) for k in range(KD) for a, b in ((xn_hi[0], w["wv_hi"]), (xn_lo[0], w["wv_hi"]), (xn_hi[0], w["wv_lo"]))]
            for kt, keys in enumerate(KEYS):
                at = image * T + kt * P
                for i, (k, a, b) in enumerate(steps):
                    mm = pe.matmul(dense[image][0:keys, kt * D:(kt + 1) * D], a[:, k, at:at + keys], b[:, k, :],
                                   start=(i == 0), stop=(i == len(steps) - 1))
            mm.then_inc(v_mm_done.sem, 1)

        def scores(c, f):
            image, r = divmod(f, 12)
            if f == 0:
                pe.wait_ge(stack_loaded.sem, stack_loaded.all(c))
                if there(c - 1):
                    pe.wait_ge(o_ready.sem, o_ready.all(c - 1))
                    pe.wait_ge(exp_far.sem, exp_far.all(c - 1))
            if f >= 2:
                pe.wait_ge(max_done.sem, max_done.count(c, f - 1))
            else:
                if there(c - 1):
                    pe.wait_ge(max_done.sem, max_done.all(c - 1))
            if r < 4:
                qt, heads = 0, range(4 * r, 4 * r + 4)
            else:
                qt, heads = 1, range(2 * (r - 4), 2 * (r - 4) + 2)
            keys = Q * (qt + 1)
            bank = score[f % 2][0:Q, 0:len(heads) * keys]
            diagonal = bank.rearrange("q (h k) -> q h k", h=len(heads))[:, :, keys - Q:keys]
            pe.matmul(diagonal, w["ident_bf"][:, :], w["mask_bf"][:, 0:len(heads) * Q].rearrange("q (h k) -> q h k", h=len(heads)),
                      start=True, stop=False, skip_group_check=True)
            at = image * T
            for i, h in enumerate(heads):
                mm = pe.matmul(bank[:, i * keys:(i + 1) * keys], q_stack[0:ROWS, h, at + qt * Q:at + (qt + 1) * Q],
                               k_stack[0:ROWS, h, at:at + keys], start=False, stop=(i == len(heads) - 1),
                               skip_group_check=True)
            mm.then_inc(fill_done.sem, 1)

        def turn_max(c):
            value0 = known(pe, max_done.all(c))
            value1 = known(pe, o_ready.all(c - 1)) if there(c - 1) else 0
            pe.wait_ge(const_done.sem, CONSTS)
            pe.wait_ge(max_done.sem, value0)
            if there(c - 1):
                pe.wait_ge(o_ready.sem, value1)
            pe.transpose(value_bank[0:HEADS * TILES, 0:Q], negmax[:, :, :].rearrange("q h t -> q (h t)"),
                         w["ident"][:, :]).then_inc(max_turned.sem, 1)

        def scores_t(c, i):
            quad, image = divmod(i, PER)
            at = image * T
            if i == 0:
                pe.wait_ge(guard_loaded.sem, guard_loaded.all(c))
            for pair in range(2):
                unit = 2 * i + pair
                if unit >= 3:
                    pe.wait_ge(exp_far.sem, exp_far.count(c, unit - 2))
                for j in range(2):
                    h = 4 * quad + 2 * pair + j
                    mm = pe.matmul(far_banks[unit % 3][:, j * T:(j + 1) * T], k_stack[:, h, at:at + P], q_stack[:, h, at:at + T],
                                   start=True, stop=True)
                mm.then_inc(far_done.sem, 1)
            if i > 0:
                pe.wait_ge(exp_near.sem, exp_near.count(c, i))
            else:
                pe.wait_ge(h_ready.sem, h_ready.all(min(c + 1, CHUNKS - 1) if isinstance(c, int) else c + 1))
            for j in range(4):
                h = 4 * quad + j
                mm = pe.matmul(near[0:KEYS[1], j * KEYS[1]:(j + 1) * KEYS[1]], k_stack[:, h, at + P:at + T],
                               q_stack[:, h, at + P:at + T], start=True, stop=True)
            mm.then_inc(near_done.sem, 1)

        def weigh(c, i):
            quad, image = divmod(i, PER)
            bank = value_banks[quad % 2]
            if i == 0:
                pe.wait_ge(v_ready.sem, v_ready.all(c))
                pe.wait_ge(guard_rest_done.sem, guard_rest_done.all(c))
            if quad >= 2:
                pe.wait_ge(o_ready.sem, o_ready.count(c, quad - 1))
            pe.wait_ge(masked_done.sem, masked_done.count(c, 2 * i + 2))
            for j in range(4):
                pe.matmul(bank[32 * j:32 * j + 32, image * T:(image + 1) * T], values[:, image, 0, 4 * quad + j, :],
                          e_far[:, i % E_SLOTS, j, :], start=True, stop=False, skip_group_check=True)
            for j in range(4):
                mm = pe.matmul(bank[32 * j:32 * j + 32, image * T + P:(image + 1) * T], values[:, image, 1, 4 * quad + j, :],
                               e_near[:, i % E_SLOTS, j, :], start=False, stop=True, skip_group_check=True)
            mm.then_inc(pv_done.sem, 1)

        def project_out(b, u, front, tok):
            if tok and u == 0:
                pe.wait_ge(h_ready.sem, h_ready.count(b + 3, 1))
            elif front:
                pe.wait_ge(qk_ready.sem, qk_ready.count(b + 2, 3 + u))
            elif there(b - 1):
                pe.wait_ge(scaled_done.sem, scaled_done.count(b - 1, u + 1))
            if u == 0:
                pe.wait_ge(y_hi_done.sem, y_hi_done.all(b))
                pe.wait_ge(y_lo_done.sem, y_lo_done.all(b))
            steps = [(k, a, v) for k in range(KD) for a, v in ((y_hi, w["wc_hi"]), (y_lo, w["wc_hi"]), (y_hi, w["wc_lo"]))]
            for t in (2 * u, 2 * u + 1):
                for i, (k, a, v) in enumerate(steps):
                    mm = pe.matmul(dense[u][0:Q, (t % 2) * D:(t % 2 + 1) * D], a[:, k, t * Q:(t + 1) * Q], v[:, k, :],
                                   start=(i == 0), stop=(i == len(steps) - 1))
            mm.then_inc(proj_done.sem, 1)

        def ffn_up(b, m):
            if m >= 4:
                pe.wait_ge(gelu_done.sem, gelu_done.count(b, m - 3))
            if m == 0:
                pe.wait_ge(xn_hi_done[1].sem, xn_hi_done[1].all(b))
                pe.wait_ge(xn_lo_done[1].sem, xn_lo_done[1].all(b))
                pe.wait_ge(exp_far.sem, exp_far.all(min(b + 1, CHUNKS - 1) if isinstance(b, int) else b + 1))
            steps = [(k, v) for k in range(KD) for v in (xn_hi[1], xn_lo[1])]
            for i, (k, v) in enumerate(steps):
                mm = pe.matmul(up_banks[m % 4][:, 0:N], w["sign1"][:, k, m * P:(m + 1) * P], v[:, k, :],
                               start=(i == 0), stop=(i == len(steps) - 1))
            mm.then_inc(up_done.sem, 1)

        def ffn_down(b, u):
            pe.wait_ge(gelu_done.sem, gelu_done.count(b, KH - 1 + u))
            for t in (2 * u, 2 * u + 1):
                for m in range(KH):
                    if t == 0:
                        pe.wait_ge(g_hi_done.sem, g_hi_done.count(b, m + 1))
                        lo = g_lo_odd if m % 2 else g_lo_even
                        pe.wait_ge(lo.sem, lo.count(b, m // 2 + 1))
                    for a in (g_hi, g_lo):
                        mm = pe.matmul(dense[u][0:Q, (t % 2) * D:(t % 2 + 1) * D], a[:, m, t * Q:(t + 1) * Q], w["sign2"][:, m, :],
                                       start=(m == 0 and a is g_hi), stop=(m == KH - 1 and a is g_lo))
            mm.then_inc(down_done.sem, 1)

        def body(c, attend=True, front=True, tok=True, prefetch=True, ffn=True):
            n, m, b = c + 1, c + 2, c - 1
            if attend:
                for f in range(FILLS):
                    scores(c, f)
                    if front and f == 3:
                        turn_front(n)
                    if front and f in (7, 10, 13, 16):
                        project_qk(n, (f - 7) // 3)
                turn_max(c)
            if tok:
                for piece in range(4):
                    tokens(m, piece)
            if attend:
                for i in range(G):
                    if i >= E_SLOTS:
                        weigh(c, i - E_SLOTS)
                    scores_t(c, i)
                    if ffn and i == 5:
                        project_out(b, 0, front, tok)
                        project_out(b, 1, front, tok)
                for i in range(G - E_SLOTS, G):
                    weigh(c, i)
            elif ffn:
                project_out(b, 0, front, tok)
                project_out(b, 1, front, tok)
            if front:
                project_v(n, 0, ffn)
                project_v(n, 1, ffn)
            if ffn:
                turn_ffn(b, front)
            if tok:
                for piece in range(4, 8):
                    tokens(m, piece)
            if ffn:
                for k in range(KH):
                    ffn_up(b, k)
                ffn_down(b, 0)
                ffn_down(b, 1)

        pe.wait_ge(const_done.sem, const_done.count(0, CONSTS))
        for piece in range(8):
            tokens(0, piece)
        turn_front(0)
        for k in range(4):
            project_qk(0, k)
        for piece in range(8):
            tokens(1, piece)
        project_v(0, 0, False)
        project_v(0, 1, False)
        body(0, ffn=False)
        body(1)
        with pe.Fori(2, CHUNKS - 3) as c:
            body(c)
        body(CHUNKS - 3, prefetch=False)
        body(CHUNKS - 2, prefetch=False, tok=False)
        body(CHUNKS - 1, prefetch=False, tok=False, front=False)
        body(CHUNKS, prefetch=False, tok=False, front=False, attend=False)

    @block.scalar
    def _(act):
        def split_x(m):
            act.wait_ge(x_loaded.sem, x_loaded.all(m))
            if there(m - 1):
                act.wait_ge(tok_done.sem, tok_done.all(m - 1))
            for half in range(2):
                at = slice(half * KF // 2, (half + 1) * KF // 2)
                act.copy(x_hi[:, at, :], x_raw[:, at, :]).then_inc(x_hi_done.sem, 1)

        def keep_h(n, u):
            act.wait_ge(tok_done.sem, tok_done.count(n, u + 1))
            if u == 0 and there(n - 1):
                act.wait_ge(xn_done[0].sem, xn_done[0].all(n - 1))
                act.wait_ge(in_next.sem, in_next.all(n - 1))
            act.copy(h_new[:, 2 * u:2 * u + 2, :].rearrange("q t d -> q (t d)"),
                     token_banks[u][0:Q, 0:2 * D]).then_inc(h_ready.sem, 1)

        def move_to_next(n):
            act.wait_ge(h_ready.sem, h_ready.all(n))
            if there(n - 1):
                act.wait_ge(in_now.sem, in_now.all(n - 1))
            act.copy(h_next[:, :, :], h_new[:, :, :]).then_inc(in_next.sem, 1)

        def move_to_now(c):
            act.wait_ge(in_next.sem, in_next.all(c))
            if there(c - 1):
                act.wait_ge(in_h1.sem, in_h1.all(c - 1))
            act.copy(h_now[:, :, :], h_next[:, :, :]).then_inc(in_now.sem, 1)

        def move_to_h1(b):
            act.wait_ge(in_now.sem, in_now.all(b))
            if there(b - 1):
                act.wait_ge(out_stored.sem, out_stored.all(b - 1))
            act.copy(h1[:, :, :], h_now[:, :, :]).then_inc(in_h1.sem, 1)

        def split_turned(i, n):
            if i == 0:
                if there(n - 1):
                    act.wait_ge(qk_mm_done.sem, qk_mm_done.all(n - 1))
                if there(n - 1):
                    act.wait_ge(v_mm_done.sem, v_mm_done.all(n - 1))
            else:
                if there(n - 1):
                    act.wait_ge(up_done.sem, up_done.all(n - 1))
            for k in range(KD):
                act.wait_ge(turn_done[i].sem, turn_done[i].count(n, k + 1))
                act.copy(xn_hi[i][:, k, :], dense[k][:, 0:N]).then_inc(xn_hi_done[i].sem, 1)

        def keep_qk(n, m):
            act.wait_ge(qk_mm_done.sem, qk_mm_done.count(n, m + 1))
            if m == 0:
                if there(n - 1):
                    act.wait_ge(part2_done.sem, part2_done.all(n - 1))
            act.copy(qk[:, m, :], dense[m % 2][:, 0:N]).then_inc(qk_ready.sem, 1)

        def keep_v(n, image):
            act.wait_ge(v_mm_done.sem, v_mm_done.count(n, image + 1))
            if there(n - 1):
                act.wait_ge(pv_done.sem, pv_done.all(n - 1))
            for kt, keys in enumerate(KEYS):
                act.copy(values[0:keys, image, kt, :, 0:DH],
                         dense[image][0:keys, kt * D:(kt + 1) * D].rearrange("k (h d) -> k h d", h=HEADS)).then_inc(v_ready.sem, 1)

        def exps(c, i):
            if i >= E_SLOTS:
                act.wait_ge(pv_done.sem, pv_done.count(c, i - E_SLOTS + 1))
            elif there(c - 1):
                act.wait_ge(pv_done.sem, pv_done.all(c - 1))
            for pair in range(2):
                act.wait_ge(far_done.sem, far_done.count(c, 2 * i + pair + 1))
                act.activation(e_far[:, i % E_SLOTS, 2 * pair:2 * pair + 2, :].rearrange("k h q -> k (h q)"),
                               far_banks[(2 * i + pair) % 3][:, 0:2 * T],
                               ACT.Exp).then_inc(exp_far.sem, 1)
            act.wait_ge(near_done.sem, near_done.count(c, i + 1))
            act.activation(e_near[0:KEYS[1], i % E_SLOTS, :, :].rearrange("k h q -> k (h q)"), near[0:KEYS[1], 0:4 * KEYS[1]],
                           ACT.Exp).then_inc(exp_near.sem, 1)

        def gelus(b):
            for m in range(KH):
                act.wait_ge(up_done.sem, up_done.count(b, m + 1))
                if m == 0:
                    act.wait_ge(y_lo_done.sem, y_lo_done.all(b))
                lo = g_lo_odd if m % 2 else g_lo_even
                if m >= G_SLOTS:
                    act.wait_ge(g_hi_done.sem, g_hi_done.count(b, m - G_SLOTS + 1))
                    act.wait_ge(lo.sem, lo.count(b, (m - G_SLOTS) // 2 + 1))
                elif there(b - 1):
                    act.wait_ge(g_hi_done.sem, g_hi_done.all(b - 1))
                    act.wait_ge(lo.sem, lo.all(b - 1))
                act.activation(g[:, m % G_SLOTS, :], up_banks[m % 4][:, 0:N], ACT.Gelu, bias=w["b1"][:, m:m + 1],
                               scale=w["alpha1"][:, m:m + 1]).then_inc(gelu_done.sem, 1)

        def split_y(c):
            act.wait_ge(y_done.sem, y_done.all(c))
            if there(c - 1):
                act.wait_ge(proj_done.sem, proj_done.all(c - 1))
            act.copy(y_hi[:, :, :], y[:, :, :]).then_inc(y_hi_done.sem, 1)

        def keep_sums(c, quad):
            act.wait_ge(pv_done.sem, pv_done.count(c, 2 * quad + 2))
            if quad == 0 and there(c - 1):
                act.wait_ge(y_loaded.sem, y_loaded.all(c - 1))
            act.copy(o_sums[:, quad, :], value_banks[quad % 2][:, 0:N]).then_inc(o_ready.sem, 1)

        def body(c, attend=True, front=True, tok=True, prefetch=True, ffn=True):
            n, m, b = c + 1, c + 2, c - 1
            if tok:
                split_x(m)
            if front:
                split_turned(0, n)
            if ffn:
                move_to_h1(b)
            if attend:
                move_to_now(c)
            if front:
                move_to_next(n)
                for k in range(4):
                    keep_qk(n, k)
            if tok:
                keep_h(m, 0)
            if attend:
                for i in range(G):
                    exps(c, i)
                    if i in (3, 5, 7):
                        keep_sums(c, (i - 3) // 2)
                    if ffn and i == 4:
                        split_y(b)
                keep_sums(c, QUADS - 1)
            elif ffn:
                split_y(b)
            if front:
                keep_v(n, 0)
                keep_v(n, 1)
            if ffn:
                split_turned(1, b)
            if tok:
                keep_h(m, 1)
            if ffn:
                gelus(b)

        split_x(0)
        keep_h(0, 0)
        keep_h(0, 1)
        split_x(1)
        split_turned(0, 0)
        act.wait_ge(const_done.sem, const_done.count(0, CONSTS))
        for k in range(4):
            keep_qk(0, k)
        move_to_next(0)
        keep_h(1, 0)
        keep_h(1, 1)
        keep_v(0, 0)
        keep_v(0, 1)
        body(0, ffn=False)
        body(1)
        with act.Fori(2, CHUNKS - 3) as c:
            body(c)
        body(CHUNKS - 3, prefetch=False)
        body(CHUNKS - 2, prefetch=False, tok=False)
        body(CHUNKS - 1, prefetch=False, tok=False, front=False)
        body(CHUNKS, prefetch=False, tok=False, front=False, attend=False)

    @block.vector
    def _(dve):
        SWAP = [p ^ 16 for p in range(32)]

        def moments_of(i, n, h):
            for t in range(TILES):
                dve.bn_stats(stats[i][:, t, :], h[:, t, :]).then_inc(stats_done[i].sem, 1)
            for t in range(TILES):
                value = known(dve, stats_done[i].count(n, t + 1))
                dve.wait_ge(const_done.sem, CONSTS)
                dve.wait_ge(stats_done[i].sem, value)
                dve.bn_aggr(moments[i][:, t, :], stats[i][:, t, :]).then_inc(moments_done[i].sem, 1)
            dve.wait_ge(moments_done[i].sem, moments_done[i].all(n))
            if there(n - 1):
                dve.wait_ge(rstd_done[i].sem, rstd_done[i].all(n - 1))
            dve.tensor_scalar(shifted[i][:, :], moments[i][:, :, 1], EPS, None, ALU.add).then_inc(shifted_done[i].sem, 1)

        def normalise(i, n, h):
            dve.wait_ge(rstd_done[i].sem, rstd_done[i].all(n))
            if there(n - 1):
                dve.wait_ge(turn_done[i].sem, turn_done[i].all(n - 1))
            if i == 1 and there(n - 1):
                dve.wait_ge(out_ready.sem, out_ready.all(n - 1))
            for t in range(TILES):
                ins = dve.tensor_scalar(xn[i][:, t, :], h[:, t, :], moments[i][:, t, 0:1], rstd[i][:, t:t + 1],
                                        ALU.subtract, ALU.mult)
            ins.then_inc(xn_done[i].sem, 1)

        def split_turned(i, n):
            for k in range(KD):
                dve.wait_ge(xn_hi_done[i].sem, xn_hi_done[i].count(n, k + 1))
                dve.tensor_tensor(xn_lo[i][:, k, :], dense[k][:, 0:N], seen(xn_hi[i][:, k, :]), ALU.subtract).then_inc(xn_lo_done[i].sem, 1)

        def residual(b):
            dve.wait_ge(in_h1.sem, in_h1.all(b))
            for u in range(2):
                dve.wait_ge(proj_done.sem, proj_done.count(b, u + 1))
                at = slice(2 * u, 2 * u + 2)
                dve.tensor_tensor(h1[:, at, :].rearrange("q t d -> q (t d)"), dense[u][0:Q, 0:2 * D],
                                  h1[:, at, :].rearrange("q t d -> q (t d)"), ALU.add).then_inc(h1_ready.sem, 1)
            dve.wait_ge(h1_ready.sem, h1_ready.all(b))

        def row_max(c, f):
            image, r = divmod(f, 12)
            dve.wait_ge(fill_done.sem, fill_done.count(c, f + 1))
            if f == 0:
                if there(c - 1):
                    dve.wait_ge(max_turned.sem, max_turned.all(c - 1))
            if r < 4:
                qt, heads = 0, slice(4 * r, 4 * r + 4)
            else:
                qt, heads = 1, slice(2 * (r - 4), 2 * (r - 4) + 2)
            count, keys = heads.stop - heads.start, Q * (qt + 1)
            dve.tensor_reduce(negmax[:, heads, 2 * image + qt], score[f % 2][0:Q, 0:count * keys].rearrange("q (h k) -> q h k", h=count),
                              AX.X, ALU.max, negate=True).then_inc(max_done.sem, 1)

        def split_guard(c):
            dve.wait_ge(max_turned.sem, max_turned.all(c))
            if there(c - 1):
                dve.wait_ge(guard_loaded.sem, guard_loaded.all(c - 1))
            src = value_bank[0:HEADS * TILES, 0:Q]
            dve.tensor_copy(guard[:, 0, :], src).then_inc(guard_split.sem, 1)
            dve.wait_ge(guard_split.sem, guard_split.count(c, 1))
            dve.tensor_tensor(guard_rest[:, :], src, guard[:, 0, :], ALU.subtract).then_inc(guard_rest_done.sem, 1)
            dve.wait_ge(guard_rest_done.sem, guard_rest_done.count(c, 1))
            dve.tensor_copy(guard[:, 1, :], guard_rest[:, :]).then_inc(guard_split.sem, 1)
            dve.wait_ge(guard_split.sem, guard_split.count(c, 2))
            dve.tensor_tensor(guard[:, 2, :], guard_rest[:, :], guard[:, 1, :], ALU.subtract).then_inc(guard_split.sem, 1)
            dve.wait_ge(guard_split.sem, guard_split.count(c, 3))
            dve.memset(guard_rest[0:1, 0:1], 0.0).then_inc(guard_rest_done.sem, 1)

        def swap(n, side):
            ready = known(dve, qk_ready.count(n, 2 * side + 2))
            summed = known(dve, rope_done.all(n - 1)) if side == 0 and there(n - 1) else None
            dve.wait_ge(const_done.sem, CONSTS)
            dve.wait_ge(qk_ready.sem, ready)
            if summed is not None:
                dve.wait_ge(rope_done.sem, summed)
            dve.stream_shuffle(turned[:, side, :], qk[:, 2 * side + 1, :], SWAP).then_inc(swapped_done.sem, 1)

        def rotate(n, side):
            dve.wait_ge(cos_done.sem, cos_done.count(n, side + 1))
            dve.wait_ge(sin_done.sem, sin_done.count(n, side + 1))
            dve.tensor_tensor(qk[:, 2 * side + 1, :], qk[:, 2 * side + 1, :], turned[:, side, :], ALU.add).then_inc(rope_done.sem, 1)

        def split_qk(n, side):
            at = slice(2 * side, 2 * side + 2)
            dve.wait_ge(rope_done.sem, rope_done.count(n, side + 1))
            if side == 0:
                if there(n - 1):
                    dve.wait_ge(stack_loaded.sem, stack_loaded.all(n - 1))
            dve.tensor_copy(part[0][:, at, :], qk[:, at, :]).then_inc(part0_done.sem, 1)
            dve.wait_ge(part0_done.sem, part0_done.count(n, side + 1))
            dve.tensor_tensor(qk[:, at, :], qk[:, at, :], part[0][:, at, :], ALU.subtract).then_inc(rest_done.sem, 1)
            dve.wait_ge(rest_done.sem, rest_done.count(n, side + 1))
            dve.tensor_copy(part[1][:, at, :], qk[:, at, :]).then_inc(part1_done.sem, 1)
            dve.wait_ge(part1_done.sem, part1_done.count(n, side + 1))
            dve.tensor_tensor(part[2][:, at, :], qk[:, at, :], part[1][:, at, :], ALU.subtract).then_inc(part2_done.sem, 1)

        def divide(c):
            dve.wait_ge(y_loaded.sem, y_loaded.all(c))
            dve.reciprocal(den[:, :, :], den[:, :, :]).then_inc(recip_done.sem, 1)
            dve.wait_ge(recip_done.sem, recip_done.all(c))
            dve.tensor_tensor(y[:, :, :], y[:, :, :], den[:, :, :], ALU.mult).then_inc(y_done.sem, 1)

        def split_g(b):
            for m in range(KH):
                dve.wait_ge(gelu_done.sem, gelu_done.count(b, m + 1))
                if m == 0:
                    if there(b - 1):
                        dve.wait_ge(down_done.sem, down_done.all(b - 1))
                dve.tensor_copy(g_hi[:, m, :], g[:, m % G_SLOTS, :]).then_inc(g_hi_done.sem, 1)
                if m % 2:
                    dve.wait_ge(g_hi_done.sem, g_hi_done.count(b, m + 1))
                    dve.tensor_tensor(g_lo[:, m, :], g[:, m % G_SLOTS, :], seen(g_hi[:, m, :]), ALU.subtract).then_inc(g_lo_odd.sem, 1)

        def scale(b):
            for u in range(2):
                dve.wait_ge(down_done.sem, down_done.count(b, u + 1))
                dve.tensor_tensor(xn[1][:, 2 * u:2 * u + 2, :], dense[u][0:Q, 0:2 * D].rearrange("q (t d) -> q t d", t=2),
                                  w["alpha2"][:, :].unsqueeze(1).to_broadcast([Q, 2, D]), ALU.mult).then_inc(scaled_done.sem, 1)

        def body(c, attend=True, front=True, tok=True, prefetch=True, ffn=True):
            n, m, b = c + 1, c + 2, c - 1
            if attend:
                for f in range(FILLS):
                    row_max(c, f)
                    if front and f == 5:
                        split_turned(0, n)
                    if front and f == 13:
                        swap(n, 0)
                    if front and f == 20:
                        swap(n, 1)
                split_guard(c)
            if ffn:
                divide(b)
            if front:
                rotate(n, 0)
                split_qk(n, 0)
            if ffn:
                residual(b)
                moments_of(1, b, h1)
            if front:
                rotate(n, 1)
                split_qk(n, 1)
            if ffn:
                normalise(1, b, h1)
                split_turned(1, b)
                split_g(b)
            if tok:
                dve.wait_ge(h_ready.sem, h_ready.all(m))
                moments_of(0, m, h_new)
                normalise(0, m, h_new)
            if ffn:
                scale(b)

        dve.memset(k_stack[ROWS:ROWS + GUARD, :, :], 1.0).then_inc(const_done.sem, 1)
        dve.memset(values[:, :, 1, :, :], 0.0).then_inc(const_done.sem, 1)
        dve.memset(e_near[:, :, :, :], 0.0).then_inc(const_done.sem, 1)
        dve.memset(values[:, :, 0, :, DH:2 * DH], 1.0).then_inc(const_done.sem, 1)
        dve.wait_ge(const_done.sem, const_done.count(0, 2))
        dve.memset(values[0:KEYS[1], :, 1, :, DH:2 * DH], 1.0).then_inc(const_done.sem, 1)
        dve.wait_ge(h_ready.sem, h_ready.all(0))
        moments_of(0, 0, h_new)
        normalise(0, 0, h_new)
        split_turned(0, 0)
        for side in range(2):
            swap(0, side)
            rotate(0, side)
            split_qk(0, side)
        dve.wait_ge(h_ready.sem, h_ready.all(1))
        moments_of(0, 1, h_new)
        normalise(0, 1, h_new)
        body(0, ffn=False)
        body(1)
        with dve.Fori(2, CHUNKS - 3) as c:
            body(c)
        body(CHUNKS - 3, prefetch=False)
        body(CHUNKS - 2, prefetch=False, tok=False)
        body(CHUNKS - 1, prefetch=False, tok=False, front=False)
        body(CHUNKS, prefetch=False, tok=False, front=False, attend=False)

    @block.gpsimd
    def _(pool):
        def power(i, n):
            pool.wait_ge(shifted_done[i].sem, shifted_done[i].all(n))
            if there(n - 1):
                pool.wait_ge(xn_done[i].sem, xn_done[i].all(n - 1))
            pool.tensor_tensor(rstd[i][:, :], shifted[i][:, :], w["minus_half"][:, :], ALU.pow).then_inc(rstd_done[i].sem, 1)

        def bias(b):
            pool.wait_ge(xn_done[1].sem, xn_done[1].all(b))
            pool.tensor_tensor(h1[:, :, :], h1[:, :, :], w["b2"][:, :].unsqueeze(1).to_broadcast([Q, TILES, D]),
                               ALU.add).then_inc(h1_biased.sem, 1)

        def split_x(m, half):
            pool.wait_ge(x_hi_done.sem, x_hi_done.count(m, half + 1))
            if there(m - 1):
                pool.wait_ge(tok_done.sem, tok_done.all(m - 1))
            at = slice(half * KF // 2, (half + 1) * KF // 2)
            pool.tensor_tensor(x_lo[:, at, :], x_raw[:, at, :], seen(x_hi[:, at, :]), ALU.subtract).then_inc(x_lo_done.sem, 1)

        def times_tables(n, side):
            pool.wait_ge(swapped_done.sem, swapped_done.count(n, side + 1))
            pool.tensor_tensor(qk[:, 2 * side + 1, :], qk[:, 2 * side + 1, :], w["cos"][:, :], ALU.mult).then_inc(cos_done.sem, 1)
            pool.tensor_tensor(turned[:, side, :], turned[:, side, :], w["sin"][:, :], ALU.mult).then_inc(sin_done.sem, 1)

        def mask(c, i):
            value = known(pool, exp_far.count(c, 2 * i + 2))
            pool.wait_ge(const_done.sem, CONSTS)
            pool.wait_ge(exp_far.sem, value)
            tile = e_far[:, i % E_SLOTS, :, 0:P]
            pool.affine_select(out=tile, in_=tile, compare_op=ALU.is_ge, fill=0.0, base=0,
                               pattern=[[0, 4], [1, P]], channel_multiplier=-1).then_inc(masked_done.sem, 1)
            value = known(pool, exp_near.count(c, i + 1))
            pool.wait_ge(const_done.sem, CONSTS)
            pool.wait_ge(exp_near.sem, value)
            tile = e_near[0:KEYS[1], i % E_SLOTS, :, :]
            pool.affine_select(out=tile, in_=tile, compare_op=ALU.is_ge, fill=0.0, base=0,
                               pattern=[[0, 4], [1, KEYS[1]]], channel_multiplier=-1).then_inc(masked_done.sem, 1)

        def split_g(b):
            for m in range(0, KH, 2):
                pool.wait_ge(g_hi_done.sem, g_hi_done.count(b, m + 1))
                pool.tensor_tensor(g_lo[:, m, :], g[:, m % G_SLOTS, :], seen(g_hi[:, m, :]), ALU.subtract).then_inc(g_lo_even.sem, 1)

        def split_y(c):
            pool.wait_ge(y_hi_done.sem, y_hi_done.all(c))
            for k in range(KD):
                pool.tensor_tensor(y_lo[:, k, :], y[:, k, :], seen(y_hi[:, k, :]), ALU.subtract).then_inc(y_lo_done.sem, 1)

        def finish(b):
            pool.wait_ge(h1_biased.sem, h1_biased.all(b))
            for u in range(2):
                pool.wait_ge(scaled_done.sem, scaled_done.count(b, u + 1))
                at = slice(2 * u, 2 * u + 2)
                pool.tensor_tensor(h1[:, at, :], xn[1][:, at, :], h1[:, at, :], ALU.add).then_inc(out_ready.sem, 1)

        def body(c, attend=True, front=True, tok=True, prefetch=True, ffn=True):
            n, m, b = c + 1, c + 2, c - 1
            if tok:
                split_x(m, 0)
                split_x(m, 1)
            if front:
                times_tables(n, 0)
                times_tables(n, 1)
            if attend:
                for i in range(G):
                    mask(c, i)
                    if ffn and i == 4:
                        split_y(b)
            elif ffn:
                split_y(b)
            if ffn:
                power(1, b)
                bias(b)
                split_g(b)
            if tok:
                power(0, m)
            if ffn:
                finish(b)

        split_x(0, 0)
        split_x(0, 1)
        power(0, 0)
        split_x(1, 0)
        split_x(1, 1)
        times_tables(0, 0)
        times_tables(0, 1)
        power(0, 1)
        body(0, ffn=False)
        body(1)
        with pool.Fori(2, CHUNKS - 3) as c:
            body(c)
        body(CHUNKS - 3, prefetch=False)
        body(CHUNKS - 2, prefetch=False, tok=False)
        body(CHUNKS - 1, prefetch=False, tok=False, front=False)
        body(CHUNKS, prefetch=False, tok=False, front=False, attend=False)


def kernel(**inputs):
    import concourse.bacc as _bacc
    from concourse.bass_utils import run_bass_kernel_spmd as _run

    a = {k: np.asarray(v) for k, v in inputs.items()}
    side = SIDE // PATCH
    x = a["x"].reshape(IMAGES, CHANNELS, side, PATCH, side, PATCH).transpose(0, 1, 3, 5, 2, 4).reshape(IMAGES, T, F)
    x = x.reshape(CHUNKS, N, KF, P).transpose(0, 3, 2, 1)

    def tiles(m):
        return m.reshape(-1, P, m.shape[1]).transpose(1, 0, 2)

    down = np.stack([a[f"L0_attn_W{s}_down"].reshape(D, HEADS, LATENT).transpose(2, 1, 0) for s in "qkv"])
    up = np.stack([np.concatenate([a["L0_attn_Wq_up_c"], a["L0_attn_Wq_up_e"]], 1),
                   np.concatenate([a["L0_attn_Wk_up_c"], a["L0_attn_Wk_up_e"]], 1), a["L0_attn_Wv_up"]], 1)
    w1, w2 = a["L0_ffn_w1"], a["L0_ffn_w2"]
    inv = (1.0 / np.float32(THETA) ** (np.arange(0, DR, 2, dtype=np.float32) / np.float32(DR))).astype(np.float32)
    angle = np.arange(T, dtype=np.float32)[:, None] * np.concatenate([inv, inv])[None, :]
    cos = np.repeat(np.tile(np.cos(angle).T, (1, PER)), HEADS, axis=0)
    sin = np.repeat(np.tile(np.sin(angle).T * np.where(np.arange(DR) % 2, 1.0, -1.0)[:, None], (1, PER)), HEADS, axis=0)
    mask = np.tile(np.where(np.tril(np.ones((Q, Q), bool)), 0.0, MASKED), (1, 4))
    arrays = {
        "x_in": x, "tok_in": tiles(a["L0_tok_W"]), "down_in": down, "up_in": up, "wc_in": tiles(a["L0_attn_Wc"]),
        "w1t_in": tiles(w1.T).reshape(P, KD * HID), "w1_in": tiles(w1), "b1_in": a["L0_ffn_b1"].reshape(KH, P).T,
        "w2t_in": tiles(w2.T).reshape(P, KH * D), "b2_in": np.broadcast_to(a["L0_ffn_b2"], (Q, D)),
        "cos_in": cos.astype(np.float32), "sin_in": sin.astype(np.float32), "mask_in": mask.astype(np.float32),
        "ident_in": np.eye(Q, dtype=np.float32),
    }
    arrays = {k: np.ascontiguousarray(v) for k, v in arrays.items()}
    nc = _bacc.Bacc("TRN2", target_bir_lowering=False, num_devices=1, dynamic_dma_scratch_size=1024)
    args = [nc.dram_tensor(k, v.shape, mybir.dt.from_np(v.dtype), kind="ExternalInput").ap() for k, v in arrays.items()]
    y = nc.dram_tensor("y_out", (CHUNKS, TILES, Q, D), FP32, kind="ExternalOutput").ap()
    vit_layer(nc, *args, y)
    r = _run(nc, [arrays], core_ids=[0])
    return r.results[0]["y_out"].reshape(IMAGES, T, D)
```

```python
import math

import numpy as np

import concourse.bass as bass
from concourse import mybir
from contextlib import ExitStack

FP32 = mybir.dt.float32
FP32R = mybir.dt.float32r
BF16 = mybir.dt.bfloat16
ALU = mybir.AluOpType
ACT = mybir.ActivationFunctionType
AX = mybir.AxisListType

IMAGES, CHANNELS, SIDE, PATCH = 64, 3, 224, 16
T = (SIDE // PATCH) ** 2
F = CHANNELS * PATCH * PATCH
D = 256
HEADS, LATENT, DH = 16, 64, 16
DR = DH // 2
HID = 1024
THETA, EPS = 10000.0, 1e-5

P = 128
PER = 2
CHUNKS = IMAGES // PER
N = PER * T
Q = T // 2
TILES = N // Q
KF, KD, KH = F // P, D // P, HID // P
KEYS = (P, T - P)
COMBOS = ((0, 0), (1, 0), (2, 0), (0, 1), (1, 1), (0, 2))
ROWS = len(COMBOS) * DH
GUARD = 3
QUADS = HEADS // 4
MASKED = -1e30
INVERT_AT = 12
DOWN_AT = [2 + 21 * i // 16 for i in range(16)]
TURN_AT, TOKENS_AT = 11, 22
E_SLOTS = 3
G_SLOTS = 4


class Event:

    def __init__(self, ctx, nc, name, per):
        self.sem, self.per = ctx.enter_context(nc.semaphore(name)), per

    def count(self, chunk, k):
        return chunk * self.per + k

    def all(self, chunk):
        return (chunk + 1) * self.per


def vit_layer(nc, x_in, tok_in, down_in, up_in, wc_in, w1t_in, w1_in, b1_in, w2t_in, b2_in,
              cos_in, sin_in, mask_in, ident_in, y_out, shares):
    with ExitStack() as ctx:
        def sb(name, shape, dt=FP32):
            return ctx.enter_context(nc.sbuf_tensor(name, shape, dt))

        tok_hi, tok_lo = sb("tok_hi", [P, KF, D], FP32R), sb("tok_lo", [P, KF, D], FP32R)
        wqk_hi, wqk_lo = sb("wqk_hi", [P, KD, 2 * D], FP32R), sb("wqk_lo", [P, KD, 2 * D], FP32R)
        wv_hi, wv_lo = sb("wv_hi", [P, KD, D], FP32R), sb("wv_lo", [P, KD, D], FP32R)
        wc_hi, wc_lo = sb("wc_hi", [P, KD, D], FP32R), sb("wc_lo", [P, KD, D], FP32R)
        sign1 = sb("sign1", [P, KD, HID], FP32R)
        sign2 = sb("sign2", [P, KH, D], FP32R)
        alpha1, b1 = sb("alpha1", [P, KH]), sb("b1", [P, KH])
        alpha2, b2 = sb("alpha2", [Q, D]), sb("b2", [Q, D])
        cos, sin = sb("cos", [P, N]), sb("sin", [P, N])
        ident = sb("ident", [Q, Q])
        ident_bf, mask_bf = sb("ident_bf", [Q, Q], BF16), sb("mask_bf", [Q, 4 * Q], BF16)
        minus_half = sb("minus_half", [Q, TILES])

        x_raw = sb("x_raw", [P, KF, N])
        x_hi, x_lo = sb("x_hi", [P, KF, N], FP32R), sb("x_lo", [P, KF, N], FP32R)
        x_loaded = Event(ctx, nc, "x_loaded", 16)
        x_hi_done, x_lo_done = Event(ctx, nc, "x_hi_done", 2), Event(ctx, nc, "x_lo_done", 2)

        prepare_weights(nc, locals())
        run_chunks(nc, ctx, sb, locals())


def prepare_weights(nc, w):
    with ExitStack() as ctx:
        def sb(name, shape, dt=FP32):
            return ctx.enter_context(nc.sbuf_tensor(name, shape, dt))

        def sem(name):
            return ctx.enter_context(nc.semaphore(name))

        tok = sb("tok_raw", [P, KF, D])
        down = [sb(f"down_{s}", [2 * LATENT, HEADS // 2, D]) for s in "qkv"]
        up, up_pair = sb("up", [2 * LATENT, 3, DH]), sb("up_pair", [2 * LATENT, 3, 2 * DH])
        wc = sb("wc_raw", [P, KD, D])
        w1t, w1, w2t = sb("w1t", [P, KD * HID]), sb("w1", [P, KH, D]), sb("w2t", [P, KH * D])
        negative1, negative2 = sb("negative1", [P, KD * HID]), sb("negative2", [P, KH * D])
        abs2 = sb("abs2", [P, KH, D])
        ones = sb("ones", [P, Q])
        mask = sb("mask", [Q, 4 * Q])
        folded = [ctx.enter_context(nc.psum_tensor(f"folded{i}", [P, 512], FP32)) for i in range(6)]
        mean2 = ctx.enter_context(nc.psum_tensor("mean2", [Q, D], FP32))

        loads = [(tok, w["tok_in"]), (w1t, w["w1t_in"]), (w1, w["w1_in"]), (w2t, w["w2t_in"]),
                 (wc, w["wc_in"]), (w["b1"], w["b1_in"]), (w["b2"], w["b2_in"]), (w["cos"], w["cos_in"]),
                 (w["sin"], w["sin_in"]), (mask, w["mask_in"]), (w["ident"], w["ident_in"])]
        pair_set = sem("pair_set")
        weights_loaded, latent_loaded = sem("weights_loaded"), sem("latent_loaded")
        fold_done, ones_set, abs_done, mean_done = sem("fold_done"), sem("ones_set"), sem("abs_done"), sem("mean_done")
        hi_done, negative_done, sum_done, prep_done = sem("hi_done"), sem("negative_done"), sem("sum_done"), sem("prep_done")
        block = ctx.enter_context(nc.Block())

        @block.sync
        def _(sp):
            for s in range(3):
                sp.dma_start(down[s][:, :, :], w["down_in"][s]).then_inc(latent_loaded, 16)
            for j in range(2):
                sp.dma_start(up[j * LATENT:(j + 1) * LATENT, :, :], w["up_in"]).then_inc(latent_loaded, 16)
            for to, of in loads:
                sp.dma_start(to[tuple(slice(None) for _ in to.shape)], of).then_inc(weights_loaded, 16)
            sp.dma_start(w["x_raw"][:, :, :], w["x_in"][0]).then_inc(w["x_loaded"].sem, 16)

        halves = [slice(half * KF // 2, (half + 1) * KF // 2) for half in range(2)]

        @block.scalar
        def _(act):
            act.wait_ge(w["x_loaded"].sem, 16)
            for half in halves:
                act.copy(w["x_hi"][:, half, :], w["x_raw"][:, half, :]).then_inc(w["x_hi_done"].sem, 1)

        @block.gpsimd
        def _(pool):
            for count, half in enumerate(halves):
                pool.wait_ge(w["x_hi_done"].sem, count + 1)
                pool.tensor_tensor(w["x_lo"][:, half, :], w["x_raw"][:, half, :], w["x_hi"][:, half, :].bitcast(FP32),
                                   ALU.subtract).then_inc(w["x_lo_done"].sem, 1)

        @block.tensor
        def _(pe):
            pe.wait_ge(latent_loaded, 5 * 16)
            pe.wait_ge(pair_set, 5)
            for s in range(3):
                for k in range(KD):
                    for h in range(0, HEADS, 2):
                        bank = folded[2 * s + k]
                        if s < 2:
                            out = bank[:, 0:D].rearrange("p (d h) -> p d h", h=HEADS)[:, :, h:h + 2]
                            pair = up_pair[:, s, :].rearrange("p (d j) -> p d j", j=2)
                        else:
                            out, pair = bank[:, h * DH:(h + 2) * DH], up_pair[:, s, :]
                        mm = pe.matmul(out, down[s][:, h // 2, k * P:(k + 1) * P], pair, start=True, stop=True)
                    mm.then_inc(fold_done, 1)
            pe.wait_ge(ones_set, 1)
            pe.wait_ge(abs_done, 1)
            for k in range(KH):
                mm = pe.matmul(mean2[:, :], ones[:, :], abs2[:, k, :], start=(k == 0), stop=(k == KH - 1))
            mm.then_inc(mean_done, 1)

        @block.vector
        def _(dve):
            dve.memset(up_pair[:, :, :], 0.0).then_inc(pair_set, 1)
            dve.memset(ones[:, :], 1.0).then_inc(ones_set, 1)
            dve.wait_ge(pair_set, 1)
            dve.wait_ge(latent_loaded, 5 * 16)
            for j in range(2):
                rows = slice(j * LATENT, (j + 1) * LATENT)
                dve.tensor_copy(up_pair[rows, 0:2, j:2 * DH:2], up[rows, 0:2, :]).then_inc(pair_set, 1)
                dve.tensor_copy(up_pair[rows, 2, j * DH:(j + 1) * DH], up[rows, 2, :]).then_inc(pair_set, 1)
            dve.memset(w["minus_half"][:, :], -0.5)
            dve.wait_ge(weights_loaded, len(loads) * 16)
            dve.scalar_tensor_tensor(out=abs2[:, :, :].rearrange("p k d -> p (k d)"), in0=w2t[:, :], scalar=-1.0,
                                     in1=w2t[:, :], op0=ALU.mult, op1=ALU.max).then_inc(abs_done, 1)
            for n, (negative, raw) in enumerate(((negative1, w1t), (negative2, w2t))):
                dve.tensor_scalar(negative[:, :], raw[:, :], 0.0, None, ALU.is_lt).then_inc(negative_done, 1)
            for n, (negative, raw, out) in enumerate(((negative1, w1t, w["sign1"]), (negative2, w2t, w["sign2"]))):
                dve.wait_ge(negative_done, n + 1)
                dve.scalar_tensor_tensor(out=out[:, :, :].rearrange("p k d -> p (k d)"), in0=raw[:, :], scalar=0.0,
                                         in1=negative[:, :], op0=ALU.is_gt, op1=ALU.subtract).then_inc(prep_done, 1)
            dve.tensor_reduce(w["alpha1"][:, :], w1[:, :, :], AX.X, ALU.add,
                              apply_absolute_value=True).then_inc(sum_done, 1)
            dve.tensor_copy(w["ident_bf"][:, :], w["ident"][:, :]).then_inc(prep_done, 1)
            dve.tensor_copy(w["mask_bf"][:, :], mask[:, :]).then_inc(prep_done, 1)
            dve.wait_ge(sum_done, 1)
            dve.tensor_scalar(w["alpha1"][:, :], w["alpha1"][:, :], 1.0 / D, None, ALU.mult).then_inc(prep_done, 1)
            dve.tensor_copy(w["tok_hi"][:, :, :], tok[:, :, :]).then_inc(hi_done, 1)
            dve.tensor_copy(w["wc_hi"][:, :, :], wc[:, :, :]).then_inc(hi_done, 1)
            dve.wait_ge(hi_done, 1)
            dve.tensor_tensor(w["tok_lo"][:, :, :], tok[:, :, :], w["tok_hi"][:, :, :].bitcast(FP32),
                              ALU.subtract).then_inc(prep_done, 1)
            dve.wait_ge(hi_done, 2)
            dve.tensor_tensor(w["wc_lo"][:, :, :], wc[:, :, :], w["wc_hi"][:, :, :].bitcast(FP32),
                              ALU.subtract).then_inc(prep_done, 1)
            parts = []
            for s in range(3):
                for k in range(KD):
                    at = slice(s * D, (s + 1) * D) if s < 2 else slice(0, D)
                    parts.append((folded[2 * s + k][:, 0:D], DH ** -0.5 if s == 0 else 1.0,
                                  (w["wqk_hi"] if s < 2 else w["wv_hi"])[:, k, at],
                                  (w["wqk_lo"] if s < 2 else w["wv_lo"])[:, k, at]))
            for n, (psum, scale, hi, lo) in enumerate(parts):
                dve.wait_ge(fold_done, n + 1)
                dve.tensor_scalar(hi, psum, scale, None, ALU.mult).then_inc(hi_done, 1)
                dve.wait_ge(hi_done, n + 3)
                dve.scalar_tensor_tensor(out=lo, in0=psum, scalar=scale, in1=hi.bitcast(FP32),
                                         op0=ALU.mult, op1=ALU.subtract).then_inc(prep_done, 1)
            dve.wait_ge(mean_done, 1)
            dve.tensor_scalar(w["alpha2"][:, :], mean2[:, :], 1.0 / HID, None, ALU.mult).then_inc(prep_done, 1)
            dve.wait_ge(prep_done, 2 + 3 + 2 + len(parts) + 1)


def there(chunk):
    return not isinstance(chunk, int) or chunk >= 0


def known(eng, value):
    return value if isinstance(value, int) else eng.to_reg(value)


def run_chunks(nc, ctx, sb, w):
    DMA = 16

    def event(name, per):
        return Event(ctx, nc, name, per)

    x_raw, x_hi, x_lo = w["x_raw"], w["x_hi"], w["x_lo"]
    table_probe = sb("table_probe", [Q, 1])
    h_new, h_next, h_now, h1 = (sb("h_new", [Q, TILES, D]), sb("h_next", [Q, TILES, D]),
                                sb("h_now", [Q, TILES, D]), sb("h1", [Q, TILES, D]))
    stats = [sb(f"stats{i}", [Q, TILES, 6]) for i in range(2)]
    moments = [sb(f"moments{i}", [Q, TILES, 2]) for i in range(2)]
    shifted = [sb(f"shifted{i}", [Q, TILES]) for i in range(2)]
    rstd = [sb(f"rstd{i}", [Q, TILES]) for i in range(2)]
    xn = [sb(f"xn{i}", [Q, TILES, D]) for i in range(2)]
    xn_hi = [sb(f"xn_hi{i}", [P, KD, N], FP32R) for i in range(2)]
    xn_lo = [sb(f"xn_lo{i}", [P, KD, N], FP32R) for i in range(2)]
    qk = sb("qk", [P, 4, N])
    turned = sb("turned", [P, 2, N])
    part = [sb(f"part{i}", [P, 4, N], BF16) for i in range(3)]
    q_stack = sb("q_stack", [ROWS + GUARD, HEADS, N], BF16)
    k_stack = sb("k_stack", [ROWS + GUARD, HEADS, N], BF16)
    negmax = sb("negmax", [Q, HEADS, TILES])
    guard = sb("guard", [HEADS * TILES, GUARD, Q], BF16)
    guard_rest = sb("guard_rest", [HEADS * TILES, Q])
    e_far = sb("e_far", [P, E_SLOTS, 4, T])
    e_near = sb("e_near", [P, E_SLOTS, 4, KEYS[1]])
    values = sb("values", [P, PER, 2, HEADS, 2 * DH])
    o_sums = sb("o_sums", [P, QUADS, N])
    sums = sb("sums", [P, QUADS * N // 32])
    y_hi, y_lo = sb("y_hi", [P, KD, N], FP32R), sb("y_lo", [P, KD, N], FP32R)
    g = sb("g", [P, G_SLOTS, N])
    den, y = g[:, 0:KD, :], g[:, KD:2 * KD, :]
    g_hi, g_lo = sb("g_hi", [P, KH, N], FP32R), sb("g_lo", [P, KH, N], FP32R)

    def bank(name):
        return ctx.enter_context(nc.psum_tensor(name, [P, 512], FP32))

    dense = [bank("dense0"), bank("dense1")]
    score = [bank("score0"), bank("score1")]
    far = [bank("far0"), bank("far1")]
    near = bank("near")
    value_bank = bank("value_bank")
    value_banks = [value_bank, score[0]]
    max_banks = [score[0], score[1], far[0], far[1]]
    far_banks = [far[0], far[1], score[1]]
    out_banks, v_banks = [dense[1], far[1]], [score[1], near]
    turn_banks = [[near, value_bank], dense]
    qk_banks = [dense[1], score[0]]
    up_banks = [far[0], far[1], dense[0], dense[1]]

    x_loaded, x_hi_done, x_lo_done = w["x_loaded"], w["x_hi_done"], w["x_lo_done"]
    tok_done, h_ready = event("tok_done", 2), event("h_ready", 2)
    in_next, in_now = event("in_next", 1), event("in_now", 1)
    stats_done = [event(f"stats_done{i}", TILES) for i in range(2)]
    moments_done = [event(f"moments_done{i}", TILES) for i in range(2)]
    shifted_done = [event(f"shifted_done{i}", 1) for i in range(2)]
    rstd_done = [event(f"rstd_done{i}", 1) for i in range(2)]
    xn_done = [event(f"xn_done{i}", 1) for i in range(2)]
    turn_done = [event(f"turn_done{i}", KD) for i in range(2)]
    xn_hi_done = [event(f"xn_hi_done{i}", KD) for i in range(2)]
    xn_lo_done = [event(f"xn_lo_done{i}", KD) for i in range(2)]
    qk_mm_done, qk_ready = event("qk_mm_done", 4), event("qk_ready", 4)
    swapped_done, times_done, rope_done = event("swapped_done", 2), event("times_done", 4), event("rope_done", 2)
    part0_done, rest_done, part1_done, part2_done = (event("part0_done", 2), event("rest_done", 2),
                                                     event("part1_done", 2), event("part2_done", 2))
    stack_loaded = event("stack_loaded", 4 * len(COMBOS) * DMA)
    v_mm_done, v_ready = event("v_mm_done", PER), event("v_ready", PER * 2)
    FILLS = PER * (4 + 8)
    fill_done, max_done = event("fill_done", FILLS), event("max_done", FILLS)
    max_turned, guard_split, guard_rest_done, guard_loaded = (event("max_turned", 1), event("guard_split", 3),
                                                              event("guard_rest_done", 2), event("guard_loaded", GUARD * DMA))
    G = QUADS * PER
    far_done, near_done = event("far_done", 2 * G), event("near_done", G)
    exp_far, exp_near = event("exp_far", 2 * G), event("exp_near", G)
    masked_done, pv_done, o_ready = event("masked_done", 2 * G), event("pv_done", G), event("o_ready", QUADS)
    y_loaded = event("y_loaded", 8 * DMA)
    sums_loaded, shares_out, den_loaded = event("sums_loaded", 4 * DMA), event("shares_out", DMA), event("den_loaded", QUADS * DMA)
    recip_done, y_done, y_hi_done, y_lo_done = (event("recip_done", 1), event("y_done", 1),
                                                event("y_hi_done", 1), event("y_lo_done", 1))
    proj_done, h1_ready, h1_biased = event("proj_done", 2), event("h1_ready", 2), event("h1_biased", 1)
    up_done, gelu_done, g_hi_done, g_lo_even, g_lo_odd = (event("up_done", KH), event("gelu_done", KH),
                                                          event("g_hi_done", KH), event("g_lo_even", KH // 2),
                                                          event("g_lo_odd", KH // 2))
    down_done, down_kept, down_scaled, out_ready, out_stored = (event("down_done", 2), event("down_kept", 2), event("down_scaled", 2),
                                                     event("out_ready", 2), event("out_stored", DMA))
    const_done = event("const_done", 1)
    CONSTS = 5

    def seen(x):
        return x.bitcast(FP32)


    block = ctx.enter_context(nc.Block())

    @block.sync
    def _(sp):
        def load_x(m, prev):
            src = w["x_in"][m] if isinstance(m, int) else w["x_in"][bass.ds(sp.snap(m), 1)].rearrange("a p k n -> (a p) k n")
            hi_split = known(sp, x_hi_done.all(prev)) if there(prev) else 0
            lo_split = known(sp, x_lo_done.all(prev)) if there(prev) else 0
            if there(prev):
                sp.wait_ge(const_done.sem, CONSTS)
                sp.wait_ge(x_hi_done.sem, hi_split)
            if there(prev):
                sp.wait_ge(x_lo_done.sem, lo_split)
            sp.dma_start(x_raw[:, :, :], src).then_inc(x_loaded.sem, 16)

        def load_guard(c):
            for r in range(GUARD):
                value = known(sp, guard_split.count(c, r + 1))
                sp.wait_ge(const_done.sem, CONSTS)
                sp.wait_ge(guard_split.sem, value)
                sp.dma_start(q_stack[ROWS + r:ROWS + r + 1, :, :], guard[:, r, :]).then_inc(guard_loaded.sem, 16)

        def load_y(c):
            hi_split = known(sp, g_hi_done.all(c - 1)) if there(c - 1) else 0
            even_split = known(sp, g_lo_even.all(c - 1)) if there(c - 1) else 0
            odd_split = known(sp, g_lo_odd.all(c - 1)) if there(c - 1) else 0
            inverted = known(sp, shares_out.all(c - 1)) if there(c - 1) else 0
            summed = known(sp, o_ready.all(c))
            sp.wait_ge(const_done.sem, CONSTS)
            if there(c - 1):
                sp.wait_ge(shares_out.sem, inverted)
            sp.wait_ge(o_ready.sem, summed)
            for j in range(4):
                sp.dma_start(sums[32 * j:32 * j + 32, :], o_sums[32 * j + DH:32 * j + DH + 1, :, :]).then_inc(sums_loaded.sem, 16)
            sp.wait_ge(const_done.sem, CONSTS)
            if there(c - 1):
                sp.wait_ge(g_hi_done.sem, hi_split)
                sp.wait_ge(g_lo_even.sem, even_split)
                sp.wait_ge(g_lo_odd.sem, odd_split)
            for odd in range(2):
                for j in range(4):
                    rows = slice(odd * 64 + j * DH, odd * 64 + (j + 1) * DH)
                    sp.dma_start(y[rows, :, :], o_sums[32 * j:32 * j + DH, odd:QUADS:2, :]).then_inc(y_loaded.sem, 16)

        def spread_shares(c):
            ready = known(sp, recip_done.all(c))
            read = known(sp, den_loaded.all(c - 1)) if there(c - 1) else 0
            sp.wait_ge(const_done.sem, CONSTS)
            if there(c - 1):
                sp.wait_ge(den_loaded.sem, read)
            sp.wait_ge(recip_done.sem, ready)
            sp.dma_start(w["shares"][:, :], sums[:, :]).then_inc(shares_out.sem, 16)
            there_now = known(sp, shares_out.all(c))
            sp.wait_ge(const_done.sem, CONSTS)
            sp.wait_ge(shares_out.sem, there_now)
            of = w["shares"].rearrange("(j p) e -> j (p e)", j=4)
            for quad in range(QUADS):
                k, odd = divmod(quad, 2)
                sp.dma_start(den[odd * 64:(odd + 1) * 64, k, :],
                             of[:, quad * N:(quad + 1) * N].unsqueeze(1).to_broadcast([4, DH, N])).then_inc(den_loaded.sem, 16)

        def load_stack(n, c):
            far_read = known(sp, far_done.all(c)) if there(c) else 0
            near_read = known(sp, near_done.all(c)) if there(c) else 0
            sp.wait_ge(const_done.sem, CONSTS)
            if there(c):
                sp.wait_ge(far_done.sem, far_read)
            if there(c):
                sp.wait_ge(near_done.sem, near_read)
            for i, made in enumerate((part0_done, part1_done, part2_done)):
                value = known(sp, made.all(n))
                sp.wait_ge(const_done.sem, CONSTS)
                sp.wait_ge(made.sem, value)
                for r, (of_q, of_k) in enumerate(COMBOS):
                    for side, stack, of in ((0, q_stack, of_q), (1, k_stack, of_k)):
                        if of != i:
                            continue
                        for rotary in range(2):
                            row = r * DH + rotary * DR
                            sp.dma_start(stack[row:row + DR, :, :], part[i][:, 2 * side + rotary, :]).then_inc(stack_loaded.sem, 16)

        def store(b):
            dst = (w["y_out"][b] if isinstance(b, int) else w["y_out"][bass.ds(sp.snap(b), 1)].rearrange("a t p d -> (a t) p d"))
            value = known(sp, out_ready.all(b))
            sp.wait_ge(const_done.sem, CONSTS)
            sp.wait_ge(out_ready.sem, value)
            sp.dma_start(dst.rearrange("t p d -> p t d"), h1[:, :, :]).then_inc(out_stored.sem, 16)

        def body(c, attend=True, front=True, tok=True, prefetch=True, ffn=True, late=True):
            if prefetch:
                load_x(c + 3, c + 2)
            if ffn:
                spread_shares(c - 1)
            if attend:
                load_guard(c)
            if late:
                store(c - 2)
            if front:
                load_stack(c + 1, c)
            if attend:
                load_y(c)

        load_x(1, 0)
        load_x(2, 1)
        load_stack(0, -1)
        body(0, ffn=False, late=False)
        body(1, late=False)
        body(2)
        with sp.Fori(3, CHUNKS - 3) as c:
            body(c)
        body(CHUNKS - 3, prefetch=False)
        body(CHUNKS - 2, prefetch=False, tok=False)
        body(CHUNKS - 1, prefetch=False, tok=False, front=False)
        body(CHUNKS, prefetch=False, tok=False, front=False, attend=False)
        body(CHUNKS + 1, prefetch=False, tok=False, front=False, attend=False, ffn=False)
        sp.wait_ge(out_stored.sem, out_stored.all(CHUNKS - 1))

    @block.tensor
    def _(pe):
        def tokens(n, piece):
            t, half = divmod(piece, 2)
            if piece == 0:
                pe.wait_ge(x_hi_done.sem, x_hi_done.all(n))
                pe.wait_ge(x_lo_done.sem, x_lo_done.all(n))
                if there(n - 4):
                    pe.wait_ge(down_kept.sem, down_kept.count(n - 4, 1))
                elif there(n - 1):
                    pe.wait_ge(h_ready.sem, h_ready.count(n - 1, 1))
            if piece == 4 and there(n - 1):
                pe.wait_ge(qk_ready.sem, qk_ready.count(n - 1, 3))
            if piece == 4 and there(n - 3):
                pe.wait_ge(h1_ready.sem, h1_ready.count(n - 3, 1))
            steps = [(k, a, b) for k in range(KF) for a, b in ((x_hi, w["tok_hi"]), (x_lo, w["tok_hi"]), (x_hi, w["tok_lo"]))]
            for i in range(9 * half, 9 * half + 9):
                k, a, b = steps[i]
                mm = pe.matmul(dense[t // 2][0:Q, (t % 2) * D:(t % 2 + 1) * D], a[:, k, t * Q:(t + 1) * Q], b[:, k, :],
                               start=(i == 0), stop=(i == len(steps) - 1))
            if piece % 4 == 3:
                mm.then_inc(tok_done.sem, 1)

        def turn_ffn(b, front, tok):
            pe.wait_ge(xn_done[1].sem, xn_done[1].all(b))
            for k in range(KD):
                if tok:
                    pe.wait_ge(h_ready.sem, h_ready.count(b + 3, k + 1))
                elif k == 1:
                    pe.wait_ge(h1_ready.sem, h1_ready.count(b, 1))
                elif there(b - 1):
                    pe.wait_ge(down_kept.sem, down_kept.count(b - 1, 1))
                for t in range(TILES):
                    mm = pe.transpose(dense[k][:, t * Q:(t + 1) * Q], xn[1][:, t, k * P:(k + 1) * P], w["ident"][:, :])
                mm.then_inc(turn_done[1].sem, 1)

        def turn_front(n):
            pe.wait_ge(xn_done[0].sem, xn_done[0].all(n))
            for k in range(KD):
                for t in range(TILES):
                    mm = pe.transpose(turn_banks[0][k][:, t * Q:(t + 1) * Q], xn[0][:, t, k * P:(k + 1) * P], w["ident"][:, :])
                mm.then_inc(turn_done[0].sem, 1)

        def project_qk(n, m):
            if m == 0:
                pe.wait_ge(xn_hi_done[0].sem, xn_hi_done[0].all(n))
                pe.wait_ge(xn_lo_done[0].sem, xn_lo_done[0].all(n))
            if m == 0 and isinstance(n, int) and n <= 2:
                pe.wait_ge(h_ready.sem, h_ready.all(n))
            elif m == 0:
                pe.wait_ge(down_kept.sem, down_kept.all(n - 3))
            if m >= 2:
                pe.wait_ge(qk_ready.sem, qk_ready.count(n, m - 1))
            steps = [(k, a, b) for k in range(KD) for a, b in ((w["wqk_hi"], xn_hi[0]), (w["wqk_lo"], xn_hi[0]), (w["wqk_hi"], xn_lo[0]))]
            for i, (k, a, b) in enumerate(steps):
                mm = pe.matmul(qk_banks[m % 2][:, 0:N], a[:, k, m * P:(m + 1) * P], b[:, k, :],
                               start=(i == 0), stop=(i == len(steps) - 1))
            mm.then_inc(qk_mm_done.sem, 1)

        def project_v(n, image):
            if there(n - 1):
                if image == 0:
                    pe.wait_ge(exp_far.sem, exp_far.all(n - 1))
                else:
                    pe.wait_ge(exp_near.sem, exp_near.all(n - 1))
            steps = [(k, a, b) for k in range(KD) for a, b in ((xn_hi[0], w["wv_hi"]), (xn_lo[0], w["wv_hi"]), (xn_hi[0], w["wv_lo"]))]
            for kt, keys in enumerate(KEYS):
                at = image * T + kt * P
                for i, (k, a, b) in enumerate(steps):
                    mm = pe.matmul(v_banks[image][0:keys, kt * D:(kt + 1) * D], a[:, k, at:at + keys], b[:, k, :],
                                   start=(i == 0), stop=(i == len(steps) - 1))
            mm.then_inc(v_mm_done.sem, 1)

        def scores(c, f):
            image, r = divmod(f, 12)
            if f == 0:
                pe.wait_ge(stack_loaded.sem, stack_loaded.all(c))
                if there(c - 1):
                    pe.wait_ge(o_ready.sem, o_ready.all(c - 1))
                    pe.wait_ge(exp_far.sem, exp_far.all(c - 1))
                pe.wait_ge(v_ready.sem, v_ready.all(c))
            if f == 2 and there(c - 2):
                pe.wait_ge(gelu_done.sem, gelu_done.count(c - 2, 6))
            if f >= 4:
                pe.wait_ge(max_done.sem, max_done.count(c, f - 3))
            if r < 4:
                qt, heads = 0, range(4 * r, 4 * r + 4)
            else:
                qt, heads = 1, range(2 * (r - 4), 2 * (r - 4) + 2)
            keys = Q * (qt + 1)
            bank = max_banks[f % 4][0:Q, 0:len(heads) * keys]
            diagonal = bank.rearrange("q (h k) -> q h k", h=len(heads))[:, :, keys - Q:keys]
            pe.matmul(diagonal, w["ident_bf"][:, :], w["mask_bf"][:, 0:len(heads) * Q].rearrange("q (h k) -> q h k", h=len(heads)),
                      start=True, stop=False, skip_group_check=True)
            at = image * T
            for i, h in enumerate(heads):
                mm = pe.matmul(bank[:, i * keys:(i + 1) * keys], q_stack[0:ROWS, h, at + qt * Q:at + (qt + 1) * Q],
                               k_stack[0:ROWS, h, at:at + keys], start=False, stop=(i == len(heads) - 1),
                               skip_group_check=True)
            mm.then_inc(fill_done.sem, 1)

        def turn_max(c, front):
            maxima = known(pe, max_done.all(c))
            sums_kept = known(pe, o_ready.all(c - 1)) if there(c - 1) else 0
            rows_kept = known(pe, xn_lo_done[0].all(c + 1)) if front else 0
            pe.wait_ge(const_done.sem, CONSTS)
            pe.wait_ge(max_done.sem, maxima)
            if front:
                pe.wait_ge(xn_lo_done[0].sem, rows_kept)
            if there(c - 1):
                pe.wait_ge(o_ready.sem, sums_kept)
            pe.transpose(value_bank[0:HEADS * TILES, 0:Q], negmax[:, :, :].rearrange("q h t -> q (h t)"),
                         w["ident"][:, :]).then_inc(max_turned.sem, 1)

        def scores_t(c, i):
            quad, image = divmod(i, PER)
            at = image * T
            if i == 0:
                pe.wait_ge(guard_loaded.sem, guard_loaded.all(c))
            for pair in range(2):
                unit = 2 * i + pair
                if unit >= 3:
                    pe.wait_ge(exp_far.sem, exp_far.count(c, unit - 2))
                for j in range(2):
                    h = 4 * quad + 2 * pair + j
                    mm = pe.matmul(far_banks[unit % 3][:, j * T:(j + 1) * T], k_stack[:, h, at:at + P], q_stack[:, h, at:at + T],
                                   start=True, stop=True)
                mm.then_inc(far_done.sem, 1)

        def scores_t_near(c, i):
            quad, image = divmod(i, PER)
            at = image * T
            if i > 0:
                pe.wait_ge(exp_near.sem, exp_near.count(c, i))
            else:
                pe.wait_ge(v_ready.sem, v_ready.all(c))
            for j in range(4):
                h = 4 * quad + j
                mm = pe.matmul(near[0:KEYS[1], j * KEYS[1]:(j + 1) * KEYS[1]], k_stack[:, h, at + P:at + T],
                               q_stack[:, h, at + P:at + T], start=True, stop=True)
            mm.then_inc(near_done.sem, 1)

        def weigh(c, i, front):
            quad, image = divmod(i, PER)
            bank = value_banks[quad % 2]
            if i == 0:
                pe.wait_ge(v_ready.sem, v_ready.all(c))
                pe.wait_ge(guard_rest_done.sem, guard_rest_done.all(c))
            if i == PER and front:
                pe.wait_ge(qk_ready.sem, qk_ready.count(c + 1, 4))
            if quad >= 2:
                pe.wait_ge(o_ready.sem, o_ready.count(c, quad - 1))
            pe.wait_ge(masked_done.sem, masked_done.count(c, 2 * i + 2))
            for j in range(4):
                pe.matmul(bank[32 * j:32 * j + 32, image * T:(image + 1) * T], values[:, image, 0, 4 * quad + j, :],
                          e_far[:, i % E_SLOTS, j, :], start=True, stop=False, skip_group_check=True)
            for j in range(4):
                mm = pe.matmul(bank[32 * j:32 * j + 32, image * T + P:(image + 1) * T], values[:, image, 1, 4 * quad + j, :],
                               e_near[:, i % E_SLOTS, j, :], start=False, stop=True, skip_group_check=True)
            mm.then_inc(pv_done.sem, 1)

        def project_out(b, u, attend, front):
            if u == 0 and front:
                pe.wait_ge(qk_ready.sem, qk_ready.count(b + 2, 3))
            elif u == 0 and there(b - 1):
                pe.wait_ge(down_kept.sem, down_kept.all(b - 1))
            if u == 1 and attend:
                pe.wait_ge(exp_far.sem, exp_far.count(b + 1, 14))
            if u == 0:
                pe.wait_ge(y_hi_done.sem, y_hi_done.all(b))
                pe.wait_ge(y_lo_done.sem, y_lo_done.all(b))
            steps = [(k, a, v) for k in range(KD) for a, v in ((y_hi, w["wc_hi"]), (y_lo, w["wc_hi"]), (y_hi, w["wc_lo"]))]
            for t in (2 * u, 2 * u + 1):
                for i, (k, a, v) in enumerate(steps):
                    mm = pe.matmul(out_banks[u][0:Q, (t % 2) * D:(t % 2 + 1) * D], a[:, k, t * Q:(t + 1) * Q], v[:, k, :],
                                   start=(i == 0), stop=(i == len(steps) - 1))
            mm.then_inc(proj_done.sem, 1)

        def ffn_up(b, m):
            if m >= 4:
                pe.wait_ge(gelu_done.sem, gelu_done.count(b, m - 3))
            if m == 0:
                pe.wait_ge(xn_hi_done[1].sem, xn_hi_done[1].all(b))
                pe.wait_ge(xn_lo_done[1].sem, xn_lo_done[1].all(b))
                pe.wait_ge(h1_ready.sem, h1_ready.all(b))
            steps = [(k, v) for k in range(KD) for v in (xn_hi[1], xn_lo[1])]
            for i, (k, v) in enumerate(steps):
                mm = pe.matmul(up_banks[m % 4][:, 0:N], w["sign1"][:, k, m * P:(m + 1) * P], v[:, k, :],
                               start=(i == 0), stop=(i == len(steps) - 1))
            mm.then_inc(up_done.sem, 1)

        def ffn_down(b, unit):
            t, pair = divmod(unit, KH // 2)
            if unit % KH == 0:
                pe.wait_ge(gelu_done.sem, gelu_done.count(b, KH - 1 + t // 2))
            for m in (2 * pair, 2 * pair + 1):
                if t == 0:
                    pe.wait_ge(g_hi_done.sem, g_hi_done.count(b, m + 1))
                    lo = g_lo_odd if m % 2 else g_lo_even
                    pe.wait_ge(lo.sem, lo.count(b, m // 2 + 1))
                for a in (g_hi, g_lo):
                    mm = pe.matmul(dense[t // 2][0:Q, (t % 2) * D:(t % 2 + 1) * D], a[:, m, t * Q:(t + 1) * Q], w["sign2"][:, m, :],
                                   start=(m == 0 and a is g_hi), stop=(m == KH - 1 and a is g_lo))
            if unit % KH == KH - 1:
                mm.then_inc(down_done.sem, 1)

        def body(c, attend=True, front=True, tok=True, prefetch=True, ffn=True, late=True):
            n, m, b = c + 1, c + 2, c - 1
            if attend:
                for f in range(FILLS):
                    scores(c, f)
                    if late and f in DOWN_AT:
                        ffn_down(c - 2, DOWN_AT.index(f))
                    if front and f == TURN_AT:
                        turn_front(n)
                    if tok and f == TOKENS_AT:
                        tokens(m, 0)
                if tok:
                    tokens(m, 1)
                turn_max(c, front)
            elif late:
                for unit in range(16):
                    ffn_down(c - 2, unit)
            if front:
                for k in range(4):
                    project_qk(n, k)
            if attend:
                for i in range(G):
                    if i >= E_SLOTS:
                        weigh(c, i - E_SLOTS, front)
                    scores_t(c, i)
                    if tok and i == 2:
                        tokens(m, 2)
                    scores_t_near(c, i)
                    if ffn and i == G - 1:
                        project_out(b, 0, attend, front)
                        project_out(b, 1, attend, front)
                for i in range(G - E_SLOTS, G):
                    weigh(c, i, front)
            if ffn and not attend:
                project_out(b, 0, attend, front)
                project_out(b, 1, attend, front)
            if tok:
                for piece in range(3, 8):
                    tokens(m, piece)
            if front:
                project_v(n, 0)
            if ffn:
                turn_ffn(b, front, tok)
            if front:
                project_v(n, 1)
            if ffn:
                for k in range(KH):
                    ffn_up(b, k)

        for piece in range(8):
            tokens(0, piece)
        turn_front(0)
        for k in range(4):
            project_qk(0, k)
        for piece in range(8):
            tokens(1, piece)
        project_v(0, 0)
        project_v(0, 1)
        pe.wait_ge(const_done.sem, const_done.count(0, CONSTS))
        body(0, ffn=False, late=False)
        body(1, late=False)
        body(2)
        with pe.Fori(3, CHUNKS - 3) as c:
            body(c)
        body(CHUNKS - 3, prefetch=False)
        body(CHUNKS - 2, prefetch=False, tok=False)
        body(CHUNKS - 1, prefetch=False, tok=False, front=False)
        body(CHUNKS, prefetch=False, tok=False, front=False, attend=False)
        body(CHUNKS + 1, prefetch=False, tok=False, front=False, attend=False, ffn=False)

    @block.scalar
    def _(act):
        def split_x(m):
            act.wait_ge(x_loaded.sem, x_loaded.all(m))
            if there(m - 1):
                act.wait_ge(tok_done.sem, tok_done.all(m - 1))
            for half in range(2):
                at = slice(half * KF // 2, (half + 1) * KF // 2)
                act.copy(x_hi[:, at, :], x_raw[:, at, :]).then_inc(x_hi_done.sem, 1)

        def keep_h(n, u):
            act.wait_ge(tok_done.sem, tok_done.count(n, u + 1))
            if u == 0 and there(n - 1):
                act.wait_ge(xn_done[0].sem, xn_done[0].all(n - 1))
                act.wait_ge(in_next.sem, in_next.all(n - 1))
            act.copy(h_new[:, 2 * u:2 * u + 2, :].rearrange("q t d -> q (t d)"),
                     dense[u][0:Q, 0:2 * D]).then_inc(h_ready.sem, 1)

        def move_to_next(n):
            act.wait_ge(h_ready.sem, h_ready.all(n))
            if there(n - 1):
                act.wait_ge(in_now.sem, in_now.all(n - 1))
            act.copy(h_next[:, :, :], h_new[:, :, :]).then_inc(in_next.sem, 1)

        def move_to_now(c):
            act.wait_ge(in_next.sem, in_next.all(c))
            if there(c - 1):
                act.wait_ge(h1_ready.sem, h1_ready.all(c - 1))
            act.copy(h_now[:, :, :], h_next[:, :, :]).then_inc(in_now.sem, 1)

        def split_turned(i, n):
            if i == 0:
                if there(n - 1):
                    act.wait_ge(qk_mm_done.sem, qk_mm_done.all(n - 1))
                if there(n - 1):
                    act.wait_ge(v_mm_done.sem, v_mm_done.all(n - 1))
            else:
                if there(n - 1):
                    act.wait_ge(up_done.sem, up_done.all(n - 1))
            for k in range(KD):
                act.wait_ge(turn_done[i].sem, turn_done[i].count(n, k + 1))
                act.copy(xn_hi[i][:, k, :], turn_banks[i][k][:, 0:N]).then_inc(xn_hi_done[i].sem, 1)

        def keep_qk(n, m):
            act.wait_ge(qk_mm_done.sem, qk_mm_done.count(n, m + 1))
            if m == 0:
                if there(n - 1):
                    act.wait_ge(part2_done.sem, part2_done.all(n - 1))
            act.copy(qk[:, m, :], qk_banks[m % 2][:, 0:N]).then_inc(qk_ready.sem, 1)

        def keep_v(n, image):
            act.wait_ge(v_mm_done.sem, v_mm_done.count(n, image + 1))
            if there(n - 1):
                act.wait_ge(pv_done.sem, pv_done.all(n - 1))
            for kt, keys in enumerate(KEYS):
                act.copy(values[0:keys, image, kt, :, 0:DH],
                         v_banks[image][0:keys, kt * D:(kt + 1) * D].rearrange("k (h d) -> k h d", h=HEADS)).then_inc(v_ready.sem, 1)

        def exps(c, i):
            if i >= E_SLOTS:
                act.wait_ge(pv_done.sem, pv_done.count(c, i - E_SLOTS + 1))
            elif there(c - 1):
                act.wait_ge(pv_done.sem, pv_done.all(c - 1))
            for pair in range(2):
                act.wait_ge(far_done.sem, far_done.count(c, 2 * i + pair + 1))
                act.activation(e_far[:, i % E_SLOTS, 2 * pair:2 * pair + 2, :].rearrange("k h q -> k (h q)"),
                               far_banks[(2 * i + pair) % 3][:, 0:2 * T],
                               ACT.Exp).then_inc(exp_far.sem, 1)
            act.wait_ge(near_done.sem, near_done.count(c, i + 1))
            act.activation(e_near[0:KEYS[1], i % E_SLOTS, :, :].rearrange("k h q -> k (h q)"), near[0:KEYS[1], 0:4 * KEYS[1]],
                           ACT.Exp).then_inc(exp_near.sem, 1)

        def keep_down(b, u):
            act.wait_ge(down_done.sem, down_done.count(b, u + 1))
            act.copy(xn[1][:, 2 * u:2 * u + 2, :].rearrange("q t d -> q (t d)"), dense[u][0:Q, 0:2 * D]).then_inc(down_kept.sem, 1)

        def load_table(function):
            act.activation(table_probe[:, :], w["minus_half"][:, 0:1], function)

        def gelus(b):
            for m in range(KH):
                if m == 0:
                    act.wait_ge(y_hi_done.sem, y_hi_done.all(b))
                    act.wait_ge(y_lo_done.sem, y_lo_done.all(b))
                lo = g_lo_odd if m % 2 else g_lo_even
                if m >= G_SLOTS:
                    act.wait_ge(g_hi_done.sem, g_hi_done.count(b, m - G_SLOTS + 1))
                    act.wait_ge(lo.sem, lo.count(b, (m - G_SLOTS) // 2 + 1))
                elif there(b - 1):
                    act.wait_ge(g_hi_done.sem, g_hi_done.all(b - 1))
                    act.wait_ge(lo.sem, lo.all(b - 1))
                act.wait_ge(up_done.sem, up_done.count(b, m + 1))
                act.activation(g[:, m % G_SLOTS, :], up_banks[m % 4][:, 0:N], ACT.Gelu, bias=w["b1"][:, m:m + 1],
                               scale=w["alpha1"][:, m:m + 1]).then_inc(gelu_done.sem, 1)

        def keep_sums(c, quad):
            act.wait_ge(pv_done.sem, pv_done.count(c, 2 * quad + 2))
            if quad == 0 and there(c - 1):
                act.wait_ge(y_loaded.sem, y_loaded.all(c - 1))
                act.wait_ge(sums_loaded.sem, sums_loaded.all(c - 1))
            act.copy(o_sums[:, quad, :], value_banks[quad % 2][:, 0:N]).then_inc(o_ready.sem, 1)

        def body(c, attend=True, front=True, tok=True, prefetch=True, ffn=True, late=True):
            n, m, b = c + 1, c + 2, c - 1
            if tok:
                split_x(m)
            if attend:
                load_table(ACT.Exp)
            if late:
                keep_down(c - 2, 0)
            if front:
                split_turned(0, n)
            if late:
                keep_down(c - 2, 1)
            if front:
                for k in range(4):
                    keep_qk(n, k)
            if attend:
                for i in range(G):
                    exps(c, i)
                    if i in (4, 6):
                        keep_sums(c, (i - 4) // 2)
                if ffn:
                    load_table(ACT.Gelu)
                keep_sums(c, QUADS - 2)
                keep_sums(c, QUADS - 1)
                move_to_now(c)
            if front:
                move_to_next(n)
            if tok:
                keep_h(m, 0)
                keep_h(m, 1)
            if front:
                keep_v(n, 0)
            if ffn:
                split_turned(1, b)
            if front:
                keep_v(n, 1)
            if ffn:
                gelus(b)

        keep_h(0, 0)
        keep_h(0, 1)
        split_x(1)
        split_turned(0, 0)
        act.wait_ge(const_done.sem, const_done.count(0, CONSTS))
        for k in range(4):
            keep_qk(0, k)
        move_to_next(0)
        keep_h(1, 0)
        keep_h(1, 1)
        keep_v(0, 0)
        keep_v(0, 1)
        body(0, ffn=False, late=False)
        body(1, late=False)
        body(2)
        with act.Fori(3, CHUNKS - 3) as c:
            body(c)
        body(CHUNKS - 3, prefetch=False)
        body(CHUNKS - 2, prefetch=False, tok=False)
        body(CHUNKS - 1, prefetch=False, tok=False, front=False)
        body(CHUNKS, prefetch=False, tok=False, front=False, attend=False)
        body(CHUNKS + 1, prefetch=False, tok=False, front=False, attend=False, ffn=False)

    @block.vector
    def _(dve):
        SWAP = [p ^ 16 for p in range(32)]

        def moments_of(i, n, h):
            for t in range(TILES):
                dve.bn_stats(stats[i][:, t, :], h[:, t, :]).then_inc(stats_done[i].sem, 1)
            for t in range(TILES):
                value = known(dve, stats_done[i].count(n, t + 1))
                dve.wait_ge(const_done.sem, CONSTS)
                dve.wait_ge(stats_done[i].sem, value)
                dve.bn_aggr(moments[i][:, t, :], stats[i][:, t, :]).then_inc(moments_done[i].sem, 1)
            dve.wait_ge(moments_done[i].sem, moments_done[i].all(n))
            if there(n - 1):
                dve.wait_ge(rstd_done[i].sem, rstd_done[i].all(n - 1))
            dve.tensor_scalar(shifted[i][:, :], moments[i][:, :, 1], EPS, None, ALU.add).then_inc(shifted_done[i].sem, 1)

        def normalise(i, n, h):
            dve.wait_ge(rstd_done[i].sem, rstd_done[i].all(n))
            if there(n - 1):
                dve.wait_ge(turn_done[i].sem, turn_done[i].all(n - 1))
            if i == 1 and there(n - 1):
                dve.wait_ge(out_ready.sem, out_ready.all(n - 1))
            for t in range(TILES):
                ins = dve.tensor_scalar(xn[i][:, t, :], h[:, t, :], moments[i][:, t, 0:1], rstd[i][:, t:t + 1],
                                        ALU.subtract, ALU.mult)
            ins.then_inc(xn_done[i].sem, 1)

        def split_turned(i, n):
            for k in range(KD):
                dve.wait_ge(xn_hi_done[i].sem, xn_hi_done[i].count(n, k + 1))
                dve.tensor_tensor(xn_lo[i][:, k, :], turn_banks[i][k][:, 0:N], seen(xn_hi[i][:, k, :]), ALU.subtract).then_inc(xn_lo_done[i].sem, 1)

        def residual(b):
            dve.wait_ge(in_now.sem, in_now.all(b))
            if there(b - 1):
                dve.wait_ge(out_stored.sem, out_stored.all(b - 1))
            for u in range(2):
                dve.wait_ge(proj_done.sem, proj_done.count(b, u + 1))
                at = slice(2 * u, 2 * u + 2)
                dve.tensor_tensor(h1[:, at, :].rearrange("q t d -> q (t d)"), out_banks[u][0:Q, 0:2 * D],
                                  h_now[:, at, :].rearrange("q t d -> q (t d)"), ALU.add).then_inc(h1_ready.sem, 1)
            dve.wait_ge(h1_ready.sem, h1_ready.all(b))

        def row_max(c, f):
            image, r = divmod(f, 12)
            dve.wait_ge(fill_done.sem, fill_done.count(c, f + 1))
            if f == 0:
                if there(c - 1):
                    dve.wait_ge(max_turned.sem, max_turned.all(c - 1))
            if r < 4:
                qt, heads = 0, slice(4 * r, 4 * r + 4)
            else:
                qt, heads = 1, slice(2 * (r - 4), 2 * (r - 4) + 2)
            count, keys = heads.stop - heads.start, Q * (qt + 1)
            dve.tensor_reduce(negmax[:, heads, 2 * image + qt], max_banks[f % 4][0:Q, 0:count * keys].rearrange("q (h k) -> q h k", h=count),
                              AX.X, ALU.max, negate=True).then_inc(max_done.sem, 1)

        def split_guard(c):
            dve.wait_ge(max_turned.sem, max_turned.all(c))
            if there(c - 1):
                dve.wait_ge(guard_loaded.sem, guard_loaded.all(c - 1))
            src = value_bank[0:HEADS * TILES, 0:Q]
            dve.tensor_copy(guard[:, 0, :], src).then_inc(guard_split.sem, 1)
            dve.wait_ge(guard_split.sem, guard_split.count(c, 1))
            dve.tensor_tensor(guard_rest[:, :], src, guard[:, 0, :], ALU.subtract).then_inc(guard_rest_done.sem, 1)
            dve.wait_ge(guard_rest_done.sem, guard_rest_done.count(c, 1))
            dve.tensor_copy(guard[:, 1, :], guard_rest[:, :]).then_inc(guard_split.sem, 1)
            dve.wait_ge(guard_split.sem, guard_split.count(c, 2))
            dve.tensor_tensor(guard[:, 2, :], guard_rest[:, :], guard[:, 1, :], ALU.subtract).then_inc(guard_split.sem, 1)
            dve.wait_ge(guard_split.sem, guard_split.count(c, 3))
            dve.memset(guard_rest[0:1, 0:1], 0.0).then_inc(guard_rest_done.sem, 1)

        def swap(n, side):
            ready = known(dve, qk_ready.count(n, 2 * side + 2))
            summed = known(dve, rope_done.all(n - 1)) if side == 0 and there(n - 1) else None
            dve.wait_ge(const_done.sem, CONSTS)
            dve.wait_ge(qk_ready.sem, ready)
            if summed is not None:
                dve.wait_ge(rope_done.sem, summed)
            dve.stream_shuffle(turned[:, side, :], qk[:, 2 * side + 1, :], SWAP).then_inc(swapped_done.sem, 1)

        def times_tables(n, side):
            dve.wait_ge(swapped_done.sem, swapped_done.count(n, side + 1))
            dve.tensor_tensor(qk[:, 2 * side + 1, :], qk[:, 2 * side + 1, :], w["cos"][:, :], ALU.mult).then_inc(times_done.sem, 1)
            dve.tensor_tensor(turned[:, side, :], turned[:, side, :], w["sin"][:, :], ALU.mult).then_inc(times_done.sem, 1)

        def rotate(n, side):
            dve.wait_ge(times_done.sem, times_done.count(n, 2 * side + 2))
            dve.tensor_tensor(qk[:, 2 * side + 1, :], qk[:, 2 * side + 1, :], turned[:, side, :], ALU.add).then_inc(rope_done.sem, 1)

        def split_qk(n, side):
            at = slice(2 * side, 2 * side + 2)
            dve.wait_ge(rope_done.sem, rope_done.count(n, side + 1))
            if side == 0:
                if there(n - 1):
                    dve.wait_ge(stack_loaded.sem, stack_loaded.all(n - 1))
            dve.tensor_copy(part[0][:, at, :], qk[:, at, :]).then_inc(part0_done.sem, 1)
            dve.wait_ge(part0_done.sem, part0_done.count(n, side + 1))
            dve.tensor_tensor(qk[:, at, :], qk[:, at, :], part[0][:, at, :], ALU.subtract).then_inc(rest_done.sem, 1)
            dve.wait_ge(rest_done.sem, rest_done.count(n, side + 1))
            dve.tensor_copy(part[1][:, at, :], qk[:, at, :]).then_inc(part1_done.sem, 1)
            dve.wait_ge(part1_done.sem, part1_done.count(n, side + 1))
            dve.tensor_tensor(part[2][:, at, :], qk[:, at, :], part[1][:, at, :], ALU.subtract).then_inc(part2_done.sem, 1)

        def invert(c):
            dve.wait_ge(sums_loaded.sem, sums_loaded.all(c))
            dve.reciprocal(sums[:, :], sums[:, :]).then_inc(recip_done.sem, 1)

        def divide(c):
            dve.wait_ge(y_loaded.sem, y_loaded.all(c))
            dve.wait_ge(den_loaded.sem, den_loaded.all(c))
            dve.tensor_tensor(y[:, :, :], y[:, :, :], den[:, :, :], ALU.mult).then_inc(y_done.sem, 1)
            dve.wait_ge(y_done.sem, y_done.all(c))
            if there(c - 1):
                dve.wait_ge(proj_done.sem, proj_done.all(c - 1))
            dve.tensor_copy(y_hi[:, :, :], y[:, :, :]).then_inc(y_hi_done.sem, 1)
            dve.wait_ge(y_hi_done.sem, y_hi_done.all(c))
            dve.tensor_tensor(y_lo[:, :, :], y[:, :, :], seen(y_hi[:, :, :]), ALU.subtract).then_inc(y_lo_done.sem, 1)

        def split_g(b):
            for m in range(KH):
                dve.wait_ge(gelu_done.sem, gelu_done.count(b, m + 1))
                if m == 0:
                    if there(b - 1):
                        dve.wait_ge(down_done.sem, down_done.all(b - 1))
                dve.tensor_copy(g_hi[:, m, :], g[:, m % G_SLOTS, :]).then_inc(g_hi_done.sem, 1)
                if m % 2:
                    dve.wait_ge(g_hi_done.sem, g_hi_done.count(b, m + 1))
                    dve.tensor_tensor(g_lo[:, m, :], g[:, m % G_SLOTS, :], seen(g_hi[:, m, :]), ALU.subtract).then_inc(g_lo_odd.sem, 1)

        def body(c, attend=True, front=True, tok=True, prefetch=True, ffn=True, late=True):
            n, m, b = c + 1, c + 2, c - 1
            if attend:
                for f in range(FILLS):
                    row_max(c, f)
                    if ffn and f == INVERT_AT:
                        invert(b)
                    if front and f == TURN_AT + 3:
                        split_turned(0, n)
                split_guard(c)
            elif ffn:
                invert(b)
            if ffn:
                divide(b)
            if front:
                swap(n, 0)
                swap(n, 1)
                times_tables(n, 0)
                times_tables(n, 1)
            if front:
                for side in range(2):
                    rotate(n, side)
                    split_qk(n, side)
            if ffn:
                residual(b)
                moments_of(1, b, h1)
                normalise(1, b, h1)
            if tok:
                dve.wait_ge(h_ready.sem, h_ready.all(m))
                moments_of(0, m, h_new)
            if ffn:
                split_turned(1, b)
            if tok:
                normalise(0, m, h_new)
            if ffn:
                split_g(b)

        dve.memset(k_stack[ROWS:ROWS + GUARD, :, :], 1.0).then_inc(const_done.sem, 1)
        dve.memset(values[:, :, 1, :, :], 0.0).then_inc(const_done.sem, 1)
        dve.memset(e_near[:, :, :, :], 0.0).then_inc(const_done.sem, 1)
        dve.memset(values[:, :, 0, :, DH:2 * DH], 1.0).then_inc(const_done.sem, 1)
        dve.wait_ge(const_done.sem, const_done.count(0, 2))
        dve.memset(values[0:KEYS[1], :, 1, :, DH:2 * DH], 1.0).then_inc(const_done.sem, 1)
        dve.wait_ge(h_ready.sem, h_ready.all(0))
        moments_of(0, 0, h_new)
        normalise(0, 0, h_new)
        split_turned(0, 0)
        swap(0, 0)
        swap(0, 1)
        times_tables(0, 0)
        times_tables(0, 1)
        for side in range(2):
            rotate(0, side)
            split_qk(0, side)
        dve.wait_ge(h_ready.sem, h_ready.all(1))
        moments_of(0, 1, h_new)
        normalise(0, 1, h_new)
        body(0, ffn=False, late=False)
        body(1, late=False)
        body(2)
        with dve.Fori(3, CHUNKS - 3) as c:
            body(c)
        body(CHUNKS - 3, prefetch=False)
        body(CHUNKS - 2, prefetch=False, tok=False)
        body(CHUNKS - 1, prefetch=False, tok=False, front=False)
        body(CHUNKS, prefetch=False, tok=False, front=False, attend=False)
        body(CHUNKS + 1, prefetch=False, tok=False, front=False, attend=False, ffn=False)

    @block.gpsimd
    def _(pool):
        def power(i, n):
            pool.wait_ge(shifted_done[i].sem, shifted_done[i].all(n))
            if there(n - 1):
                pool.wait_ge(xn_done[i].sem, xn_done[i].all(n - 1))
            pool.tensor_tensor(rstd[i][:, :], shifted[i][:, :], w["minus_half"][:, :], ALU.pow).then_inc(rstd_done[i].sem, 1)

        def bias(b):
            pool.wait_ge(xn_done[1].sem, xn_done[1].all(b))
            pool.tensor_tensor(h1[:, :, :], h1[:, :, :], w["b2"][:, :].unsqueeze(1).to_broadcast([Q, TILES, D]),
                               ALU.add).then_inc(h1_biased.sem, 1)

        def split_x(m, half):
            pool.wait_ge(x_hi_done.sem, x_hi_done.count(m, half + 1))
            if there(m - 1):
                pool.wait_ge(tok_done.sem, tok_done.all(m - 1))
            at = slice(half * KF // 2, (half + 1) * KF // 2)
            pool.tensor_tensor(x_lo[:, at, :], x_raw[:, at, :], seen(x_hi[:, at, :]), ALU.subtract).then_inc(x_lo_done.sem, 1)

        def mask(c, i):
            value = known(pool, exp_far.count(c, 2 * i + 2))
            pool.wait_ge(const_done.sem, CONSTS)
            pool.wait_ge(exp_far.sem, value)
            tile = e_far[:, i % E_SLOTS, :, 0:P]
            pool.affine_select(out=tile, in_=tile, compare_op=ALU.is_ge, fill=0.0, base=0,
                               pattern=[[0, 4], [1, P]], channel_multiplier=-1).then_inc(masked_done.sem, 1)
            value = known(pool, exp_near.count(c, i + 1))
            pool.wait_ge(const_done.sem, CONSTS)
            pool.wait_ge(exp_near.sem, value)
            tile = e_near[0:KEYS[1], i % E_SLOTS, :, :]
            pool.affine_select(out=tile, in_=tile, compare_op=ALU.is_ge, fill=0.0, base=0,
                               pattern=[[0, 4], [1, KEYS[1]]], channel_multiplier=-1).then_inc(masked_done.sem, 1)

        def split_g(b):
            for m in range(0, KH, 2):
                pool.wait_ge(g_hi_done.sem, g_hi_done.count(b, m + 1))
                pool.tensor_tensor(g_lo[:, m, :], g[:, m % G_SLOTS, :], seen(g_hi[:, m, :]), ALU.subtract).then_inc(g_lo_even.sem, 1)

        def finish(b):
            for u in range(2):
                pool.wait_ge(down_kept.sem, down_kept.count(b, u + 1))
                at = slice(2 * u, 2 * u + 2)
                pool.tensor_tensor(xn[1][:, at, :], xn[1][:, at, :], w["alpha2"][:, :].unsqueeze(1).to_broadcast([Q, 2, D]),
                                   ALU.mult).then_inc(down_scaled.sem, 1)
            pool.wait_ge(h1_biased.sem, h1_biased.all(b))
            for u in range(2):
                pool.wait_ge(down_scaled.sem, down_scaled.count(b, u + 1))
                at = slice(2 * u, 2 * u + 2)
                pool.tensor_tensor(h1[:, at, :], xn[1][:, at, :], h1[:, at, :], ALU.add).then_inc(out_ready.sem, 1)

        def body(c, attend=True, front=True, tok=True, prefetch=True, ffn=True, late=True):
            n, m, b = c + 1, c + 2, c - 1
            if tok:
                split_x(m, 0)
                split_x(m, 1)
            if late:
                finish(c - 2)
            if attend:
                for i in range(G):
                    mask(c, i)
            if ffn:
                power(1, b)
            if tok:
                power(0, m)
            if ffn:
                bias(b)
                split_g(b)

        power(0, 0)
        split_x(1, 0)
        split_x(1, 1)
        power(0, 1)
        body(0, ffn=False, late=False)
        body(1, late=False)
        body(2)
        with pool.Fori(3, CHUNKS - 3) as c:
            body(c)
        body(CHUNKS - 3, prefetch=False)
        body(CHUNKS - 2, prefetch=False, tok=False)
        body(CHUNKS - 1, prefetch=False, tok=False, front=False)
        body(CHUNKS, prefetch=False, tok=False, front=False, attend=False)
        body(CHUNKS + 1, prefetch=False, tok=False, front=False, attend=False, ffn=False)


def kernel(**inputs):
    import concourse.bacc as _bacc
    from concourse.bass_utils import run_bass_kernel_spmd as _run

    a = {k: np.asarray(v) for k, v in inputs.items()}
    side = SIDE // PATCH
    x = a["x"].reshape(IMAGES, CHANNELS, side, PATCH, side, PATCH).transpose(0, 1, 3, 5, 2, 4).reshape(IMAGES, T, F)
    x = x.reshape(CHUNKS, N, KF, P).transpose(0, 3, 2, 1)

    def tiles(m):
        return m.reshape(-1, P, m.shape[1]).transpose(1, 0, 2)

    down = np.stack([a[f"L0_attn_W{s}_down"].reshape(D, HEADS // 2, 2 * LATENT).transpose(2, 1, 0) for s in "qkv"])
    up = np.stack([np.concatenate([a["L0_attn_Wq_up_c"], a["L0_attn_Wq_up_e"]], 1),
                   np.concatenate([a["L0_attn_Wk_up_c"], a["L0_attn_Wk_up_e"]], 1), a["L0_attn_Wv_up"]], 1)
    w1, w2 = a["L0_ffn_w1"], a["L0_ffn_w2"]
    inv = (1.0 / np.float32(THETA) ** (np.arange(0, DR, 2, dtype=np.float32) / np.float32(DR))).astype(np.float32)
    angle = np.arange(T, dtype=np.float32)[:, None] * np.concatenate([inv, inv])[None, :]
    cos = np.repeat(np.tile(np.cos(angle).T, (1, PER)), HEADS, axis=0)
    sin = np.repeat(np.tile(np.sin(angle).T * np.where(np.arange(DR) % 2, 1.0, -1.0)[:, None], (1, PER)), HEADS, axis=0)
    mask = np.tile(np.where(np.tril(np.ones((Q, Q), bool)), 0.0, MASKED), (1, 4))
    arrays = {
        "x_in": x, "tok_in": tiles(a["L0_tok_W"]), "down_in": down, "up_in": up, "wc_in": tiles(a["L0_attn_Wc"]),
        "w1t_in": tiles(w1.T).reshape(P, KD * HID), "w1_in": tiles(w1), "b1_in": a["L0_ffn_b1"].reshape(KH, P).T,
        "w2t_in": tiles(w2.T).reshape(P, KH * D), "b2_in": np.broadcast_to(a["L0_ffn_b2"], (Q, D)),
        "cos_in": cos.astype(np.float32), "sin_in": sin.astype(np.float32), "mask_in": mask.astype(np.float32),
        "ident_in": np.eye(Q, dtype=np.float32),
    }
    arrays = {k: np.ascontiguousarray(v) for k, v in arrays.items()}
    nc = _bacc.Bacc("TRN2", target_bir_lowering=False, num_devices=1, dynamic_dma_scratch_size=1024)
    args = [nc.dram_tensor(k, v.shape, mybir.dt.from_np(v.dtype), kind="ExternalInput").ap() for k, v in arrays.items()]
    y = nc.dram_tensor("y_out", (CHUNKS, TILES, Q, D), FP32, kind="ExternalOutput").ap()
    shares = nc.dram_tensor("shares", (P, QUADS * N // 32), FP32).ap()
    vit_layer(nc, *args, y, shares)
    r = _run(nc, [arrays], core_ids=[0])
    return r.results[0]["y_out"].reshape(IMAGES, T, D)
```
